# Optimizing a Trainium2 kernel written in Bass

```python
import numpy as np
import jax
import jax.numpy as jnp

def _softmax(x, axis=-1):
    return jax.nn.softmax(x, axis=axis)

def _gelu(x):
    return jax.nn.gelu(x, approximate=True)

def _silu(x):
    return jax.nn.silu(x)

def _sigmoid(x):
    return jax.nn.sigmoid(x)

def _layernorm(x, axis=-1, eps=1e-05):
    m = jnp.mean(x, axis=axis, keepdims=True)
    v = jnp.var(x, axis=axis, keepdims=True)
    return (x - m) / jnp.sqrt(v + eps)

def _scatter_add(tgt, idx, src, axis=0):
    return tgt.at[idx].add(src)

def _segment_sum(src, seg, n):
    return jax.ops.segment_sum(src, seg, n)
kernel_name = 'mk_cond_resid_d2_seqx_r4_3406df'

def setup_inputs(seed: int=0):
    np.random.seed(seed)
    _w = jnp.asarray

    def _rec_inputs():
        import jax
        import jax.numpy as jnp
        _rk = jax.random.key(seed)
        x = -0.0003929 + 0.9999 * jax.random.normal(jax.random.fold_in(_rk, 1), (8, 256, 512), jnp.float32)
        _lenS = 256 - jax.random.randint(jax.random.fold_in(_rk, 7), (8,), 0, max(1, 256 // 4) + 1, jnp.int32)
        _lenS2 = 256 - jax.random.randint(jax.random.fold_in(_rk, 8), (8,), 0, max(1, 256 // 4) + 1, jnp.int32)
        cond_2048 = 0.00782532 + 1.00527 * jax.random.normal(jax.random.fold_in(_rk, 11), (8, 512), jnp.float32)
        return (x, cond_2048)
    x, cond_2048 = _rec_inputs()

    def _L0_cond_setup():
        import jax, jax.numpy as jnp
        import numpy as np
        HEADS = 16
        EPS = 1e-06

        def _rms_norm(x, g):
            xf = x.astype(jnp.float32)
            y = xf * jax.lax.rsqrt(jnp.mean(xf * xf, axis=-1, keepdims=True) + EPS)
            return y.astype(x.dtype) * g
        key = jax.random.key(seed)
        ks = jax.random.split(key, 6)
        b, n, dim, emb_dim = (4, 512, 512, 512)
        d_head = dim // HEADS
        return {'x': jax.random.normal(ks[0], (b, n, dim), jnp.float32), 'emb': jax.random.normal(ks[1], (b, 1, emb_dim), jnp.float32), 'W_emb': jax.random.normal(ks[2], (emb_dim, 2 * dim), jnp.float32) * emb_dim ** (-0.5), 'b_emb': jnp.zeros((2 * dim,), jnp.float32), 'g_norm': jnp.ones((dim,), jnp.float32), 'W_qkv': jax.random.normal(ks[3], (dim, 3 * dim), jnp.float32) * dim ** (-0.5), 'g_q': jnp.ones((d_head,), jnp.float32), 'g_k': jnp.ones((d_head,), jnp.float32), 'W_out': jax.random.normal(ks[4], (dim, dim), jnp.float32) * dim ** (-0.5)}
    _L0_cond_all = _L0_cond_setup()
    _L0_cond_in = {k: v for k, v in _L0_cond_all.items() if k in ('W_emb', 'b_emb', 'g_norm', 'W_qkv', 'g_q', 'g_k', 'W_out')}
    del _L0_cond_all

    def _L1_cond_setup():
        import math
        import jax, jax.numpy as jnp
        import numpy as np
        ENCODER_SIZE = 256
        NUM_HEADER = 16
        DK = ENCODER_SIZE // NUM_HEADER
        B, S = (4, 512)
        key = jax.random.key(seed)
        kx, km, kq, kk, kv, ko = jax.random.split(key, 6)
        x = jax.random.normal(kx, (B, ENCODER_SIZE, S), dtype=jnp.float32)
        mask = (jax.random.uniform(km, (B, S)) < 0.9).astype(jnp.float32)
        lim = math.sqrt(6.0 / (ENCODER_SIZE + DK))
        Wq = jax.random.uniform(kq, (NUM_HEADER, ENCODER_SIZE, DK), minval=-lim, maxval=lim, dtype=jnp.float32)
        Wk = jax.random.uniform(kk, (NUM_HEADER, ENCODER_SIZE, DK), minval=-lim, maxval=lim, dtype=jnp.float32)
        Wv = jax.random.uniform(kv, (NUM_HEADER, ENCODER_SIZE, DK), minval=-lim, maxval=lim, dtype=jnp.float32)
        limo = math.sqrt(6.0 / ENCODER_SIZE)
        Wo = jax.random.uniform(ko, (ENCODER_SIZE, ENCODER_SIZE), minval=-limo, maxval=limo, dtype=jnp.float32)
        return {'x': x, 'mask': mask, 'Wq': Wq, 'Wk': Wk, 'Wv': Wv, 'Wo': Wo}
    _L1_cond_all = _L1_cond_setup()
    _L1_cond_in = {k: v for k, v in _L1_cond_all.items() if k in ('Wq', 'Wk', 'Wv', 'Wo')}
    del _L1_cond_all
    return {'x': x, 'cond_2048': cond_2048, 'L0_cond_W_emb': _L0_cond_in['W_emb'], 'L0_cond_b_emb': _L0_cond_in['b_emb'], 'L0_cond_g_norm': _L0_cond_in['g_norm'], 'L0_cond_W_qkv': _L0_cond_in['W_qkv'], 'L0_cond_g_q': _L0_cond_in['g_q'], 'L0_cond_g_k': _L0_cond_in['g_k'], 'L0_cond_W_out': _L0_cond_in['W_out'], 'L1_cond_Wq': _L1_cond_in['Wq'], 'L1_cond_Wk': _L1_cond_in['Wk'], 'L1_cond_Wv': _L1_cond_in['Wv'], 'L1_cond_Wo': _L1_cond_in['Wo']}

def reference(x, cond_2048, L0_cond_W_emb, L0_cond_b_emb, L0_cond_g_norm, L0_cond_W_qkv, L0_cond_g_q, L0_cond_g_k, L0_cond_W_out, L1_cond_Wq, L1_cond_Wk, L1_cond_Wv, L1_cond_Wo):
    import jax
    import jax.numpy as jnp

    def _L0_cond_ref(x, emb, W_emb, b_emb, g_norm, W_qkv, g_q, g_k, W_out):
        import jax, jax.numpy as jnp
        import numpy as np
        HEADS = 16
        EPS = 1e-06

        def _rms_norm(x, g):
            xf = x.astype(jnp.float32)
            y = xf * jax.lax.rsqrt(jnp.mean(xf * xf, axis=-1, keepdims=True) + EPS)
            return y.astype(x.dtype) * g
        b, n, dim = x.shape
        h = HEADS
        d = dim // h
        scale_shift = emb @ W_emb + b_emb
        scale, shift = jnp.split(scale_shift, 2, axis=-1)
        xn = _rms_norm(x, g_norm) * (1.0 + scale) + shift
        qkv = xn @ W_qkv
        qkv = qkv.reshape(b, n, 3, h, d)
        q, k, v = jnp.moveaxis(qkv, 2, 0)
        q = jnp.swapaxes(q, 1, 2)
        k = jnp.swapaxes(k, 1, 2)
        v = jnp.swapaxes(v, 1, 2)
        q = _rms_norm(q, g_q)
        k = _rms_norm(k, g_k)
        logits = jnp.einsum('bhqd,bhkd->bhqk', q, k) * d ** (-0.5)
        attn = jax.nn.softmax(logits, axis=-1)
        o = jnp.einsum('bhqk,bhkd->bhqd', attn, v)
        o = jnp.swapaxes(o, 1, 2).reshape(b, n, dim)
        return o + o @ W_out

    def _L1_cond_ref(x, mask, Wq, Wk, Wv, Wo):
        import math
        import jax, jax.numpy as jnp
        import numpy as np
        ENCODER_SIZE = 256
        NUM_HEADER = 16
        DK = ENCODER_SIZE // NUM_HEADER
        B, S = (4, 512)
        num_header = Wq.shape[0]
        dk = Wq.shape[2]
        sqrt_dk_inv = 1.0 / math.sqrt(dk)
        xt = jnp.transpose(x, (0, 2, 1))
        q = xt @ Wq[1]
        k = xt @ Wk[1]
        v = xt @ Wv[1]
        scores = jnp.einsum('bqd,bkd->bqk', q, k) * sqrt_dk_inv
        hmask = mask[:, None, :]
        vmask = mask[:, :, None]
        scores = scores * hmask + (1.0 - hmask) * -1e+30
        attn = jax.nn.softmax(scores, axis=2) * vmask
        head = attn @ v
        heads = jnp.tile(head, (1, 1, num_header))
        out = heads @ Wo
        return jnp.transpose(out, (0, 2, 1))
    x = x + _L0_cond_ref(x, cond_2048[:, None, :], L0_cond_W_emb, L0_cond_b_emb, L0_cond_g_norm, L0_cond_W_qkv, L0_cond_g_q, L0_cond_g_k, L0_cond_W_out)
    x = x + _L1_cond_ref(x, cond_2048, L1_cond_Wq, L1_cond_Wk, L1_cond_Wv, L1_cond_Wo)
    return x

_drawn_inputs = setup_inputs


def setup_inputs(seed=0):
    import zlib

    import numpy as np

    out = dict(_drawn_inputs(seed))
    spreads = {'L0_cond_b_emb': (0.0, 0.1),
     'L0_cond_g_norm': (1.0, 0.2),
     'L0_cond_g_q': (1.0, 0.6),
     'L0_cond_g_k': (1.0, 0.591)}
    factors = {}
    for name, (base, spread) in spreads.items():
        noise = np.random.default_rng([zlib.crc32(name.encode()), seed]).standard_normal(out[name].shape)
        drawn = base * np.exp(spread * noise) if base else spread * noise
        out[name] = jnp.asarray(drawn.astype(out[name].dtype))
    for name, factor in factors.items():
        out[name] = (out[name] * factor).astype(out[name].dtype)
    return out
```

```python
import concourse.bass as bass
from concourse import mybir
from contextlib import ExitStack


B, N, D, H, HD = 8, 256, 512, 16, 32
P = 128
NT = N // P
KC = D // P
G = 4
NG = H // G
S1, DK = 512, 16
ET, QT = N // P, S1 // P
SHIFT_ROW = 3 * HD
EPS = 1e-6
NEG = 1e30

F32 = mybir.dt.float32
F32R = mybir.dt.float32r
ACT = mybir.ActivationFunctionType
ALU = mybir.AluOpType
AX = mybir.AxisListType


def at(batch, per_batch, more):
    return batch * per_batch + more


def wait(eng, sem, value):
    if not isinstance(value, int) or value > 0:
        eng.wait_ge(sem, value)


def settle(eng, count, batch):
    if not isinstance(batch, int):
        eng.sem_inc(count, 1)


def f32(ap):
    return ap.bitcast(F32)


def build(nc, x, cond, W_emb, b_emb, g_norm, W_qkv, g_q, g_k, W_out, L1_Wq, L1_Wk, L1_Wv, L1_Wo, out):
    ctx = ExitStack()
    with ctx:
        def sb(name, shape, dt=F32, where=ctx):
            return where.enter_context(nc.sbuf_tensor(name, shape, dt))

        def sem(name):
            return ctx.enter_context(nc.semaphore(name))

        wqkv_hi = sb("wqkv_hi", [P, KC, 3 * D], F32R)
        wqkv_lo = sb("wqkv_lo", [P, KC, 3 * D], F32R)
        wout_hi = sb("wout_hi", [P, KC, D], F32R)
        wout_lo = sb("wout_lo", [P, KC, D], F32R)
        ident = sb("ident", [P, P])
        ident_r = sb("ident_r", [P, P], F32R)
        gq_bc = sb("gq_bc", [P, HD])
        gk_bc = sb("gk_bc", [P, HD])
        gain_bc = sb("gain_bc", [P, HD])
        minus_half = sb("minus_half", [P, H])
        cond_T = sb("cond_T", [P, B, KC])
        biasgain_T = sb("biasgain_T", [P, 12])
        mod_all = sb("mod_all", [P, B, 2 * KC])
        mod_cur = sb("mod_cur", [P, 2 * KC])
        w1_in = sb("w1_in", [P, 3, ET, DK])
        wq1 = sb("wq1", [P, ET, 112])
        wk1 = sb("wk1", [P, ET, 96])
        wo1 = sb("wo1", [DK, N])

        staging = ExitStack()
        w_emb_in = sb("w_emb_in", [P, KC, 2 * D], F32, staging)
        w_qkv_in = sb("w_qkv_in", [P, KC, 3 * D], F32, staging)
        w_out_in = sb("w_out_in", [P, KC, D], F32, staging)
        wo1_in = sb("wo1_in", [DK, H, N], F32, staging)
        rows_in = sb("rows_in", [12, P], F32, staging)
        cond_in = sb("cond_in", [B, D], F32, staging)
        staging.close()

        qk_split = sb("qk_split", [P, 2, NT, H, 3 * HD], F32R)
        q_stack = sb("q_stack", [SHIFT_ROW + 1, H, N], F32R)
        k_stack = sb("k_stack", [SHIFT_ROW + 1, H, N], F32R)
        qk_raw = sb("qk_raw", [P, NT, 2, D])
        squares = sb("squares", [P, 2, D])
        head_ms = sb("head_ms", [P, 4, H])
        head_rstd = sb("head_rstd", [P, 4, H])
        x_in = sb("x_in", [P, NT, D])
        x_ms = sb("x_ms", [P, NT])
        x_rstd = sb("x_rstd", [P, NT])
        xn_T = sb("xn_T", [P, KC, N])
        xn_hi = sb("xn_hi", [P, KC, N], F32R)
        xn_lo = sb("xn_lo", [P, KC, N], F32R)
        v_one = sb("v_one", [P, NT, H, HD + 1])
        maxima = sb("maxima", [P, 2, NT, H // 2])
        shift_T = [sb(f"shift_T{k}", [H, P], F32R) for k in range(2)]
        e = [sb(f"e{k}", [P, NT, N]) for k in range(3)]
        o_rden = sb("o_rden", [P, NT, G])
        o_sb = sb("o_sb", [P, NT, D])
        o_hi = sb("o_hi", [P, KC, N], F32R)
        o_lo = sb("o_lo", [P, KC, N], F32R)
        resid = sb("resid", [P, NT, D])
        x1 = sb("x1", [P, NT, D])
        mask_bc = sb("mask_bc", [P, S1])
        pad_bias = sb("pad_bias", [P, S1])
        q1 = sb("q1", [96, S1], F32R)
        k1 = sb("k1", [96, S1], F32R)
        kv1 = sb("kv1", [112, S1])
        v1 = sb("v1", [P, QT, DK])
        e1 = [sb(f"e1_{k}", [P, S1]) for k in range(2)]
        min1 = sb("min1", [P, QT])
        sum1 = sb("sum1", [P, QT])
        row1 = sb("row1", [P, QT])
        vmask = sb("vmask", [P, QT])
        e1_T = [sb(f"e1_T{k}", [P, QT, P]) for k in range(2)]
        head1 = sb("head1", [P, QT, DK])
        head1_T = sb("head1_T", [DK, S1])

        def bank(name):
            return ctx.enter_context(nc.psum_tensor(name, [P, 512], F32))
        ps_logit = [bank(f"ps_logit{k}") for k in range(2)]
        ps_max = [bank(f"ps_max{k}") for k in range(2)]
        ps_o = [bank(f"ps_o{k}") for k in range(2)]
        ps_w = [bank(f"ps_w{k}") for k in range(2)]

        s_cond, s_rows, s_wemb, s_wout, s_wo1, s_w1, s_gains = map(
            sem, ["s_cond", "s_rows", "s_wemb", "s_wout", "s_wo1", "s_w1", "s_gains"])
        s_wqkv = [sem(f"s_wqkv{k}") for k in range(KC)]
        s_x, s_resid, s_mask, s_out = map(sem, ["s_x", "s_resid", "s_mask", "s_out"])
        s_shift = [sem(f"s_shift{k}") for k in range(2)]
        s_const, s_ident, s_condT, s_condT_sb, s_mod_ps, s_mod_b, s_mod, s_wsplit, s_w1sb, s_wo1sb, s_gain = map(
            sem, ["s_const", "s_ident", "s_condT", "s_condT_sb", "s_mod_ps", "s_mod_b", "s_mod", "s_wsplit",
                  "s_w1sb", "s_wo1sb", "s_gain"])
        s_whi, s_ones = sem("s_whi"), sem("s_ones")
        p_xT, p_qkv, p_stack, p_max, p_maxT, p_logit, p_o, p_oT, p_wout = map(
            sem, ["p_xT", "p_qkv", "p_stack", "p_max", "p_maxT", "p_logit", "p_o", "p_oT", "p_wout"])
        p_v = sem("p_v")
        p_proj1, p_vT, p_score1, p_eT, p_o1, p_headT, p_out1 = map(
            sem, ["p_proj1", "p_vT", "p_score1", "p_eT", "p_o1", "p_headT", "p_out1"])
        a_xms, a_xnT, a_raw, a_sq, a_v, a_hi, a_stack, a_e, a_ohi = map(
            sem, ["a_xms", "a_xnT", "a_raw", "a_sq", "a_v", "a_hi", "a_stack", "a_e", "a_ohi"])
        a_q1, a_vT, a_v1, a_e1, a_eT, a_headT = map(sem, ["a_q1", "a_vT", "a_v1", "a_e1", "a_eT", "a_headT"])
        v_x, v_ms, v_qkn, v_stack, v_max, v_shift, v_rden, v_o, v_olo, v_x1 = map(
            sem, ["v_x", "v_ms", "v_qkn", "v_stack", "v_max", "v_shift", "v_rden", "v_o", "v_olo", "v_x1"])
        v_q1, v_k1, v_score1, v_rsum1, v_row1, v_head1, v_x2 = map(
            sem, ["v_q1", "v_k1", "v_score1", "v_rsum1", "v_row1", "v_head1", "v_x2"])
        g_mod, g_xeps, g_xrstd, g_xhi, g_xlo, g_keps, g_rstd, g_kgain, g_split, g_resid = map(
            sem, ["g_mod", "g_xeps", "g_xrstd", "g_xhi", "g_xlo", "g_keps", "g_rstd", "g_kgain", "g_split", "g_resid"])
        g_pad0, g_pad, g_k1hi, g_k1lo, g_vmask = map(sem, ["g_pad0", "g_pad", "g_k1hi", "g_k1lo", "g_vmask"])

        passed_pool, passed_sp, passed_dve, passed_pe = map(
            sem, ["passed_pool", "passed_sp", "passed_dve", "passed_pe"])

        block = ctx.enter_context(nc.Block())

        def steps(eng, step):
            step(None, None, None, 0)
            step(None, None, 0, 1)
            step(None, 0, 1, 2)
            step(0, 1, 2, 3)
            with eng.Fori(2, B - 2) as i:
                step(i - 1, i, i + 1, i + 2)
            step(B - 3, B - 2, B - 1, None)
            step(B - 2, B - 1, None, None)
            step(B - 1, None, None, None)

        @block.sync
        def _(sp):
            sp.dma_start(cond_in[:], cond).then_inc(s_cond, 16)
            sp.dma_start(rows_in[0:8, :], b_emb.rearrange("(c p) -> c p", p=P)).then_inc(s_rows, 16)
            sp.dma_start(rows_in[8:12, :], g_norm.rearrange("(c p) -> c p", p=P)).then_inc(s_rows, 16)
            w_emb_v = W_emb.rearrange("(c p) n -> p c n", p=P)
            for c in range(KC):
                sp.dma_start(w_emb_in[:, c], w_emb_v[:, c]).then_inc(s_wemb, 16)

            def load_x(n):
                if not isinstance(n, int) or n > 0:
                    sp.wait_ge(p_xT, at(n, 2, 0))
                settle(sp, passed_sp, n)
                sp.dma_start(x_in[:], x[n].rearrange("(t p) d -> p t d", p=P)).then_inc(s_x, 16)

            def shift_rows(half, batch):
                wait(sp, v_shift, at(batch, 2, half + 1))
                settle(sp, passed_sp, batch)
                h0 = half * (H // 2)
                wait(sp, p_logit, at(batch, H, -(H // 2)) if half == 0 else at(batch, H, 0))
                settle(sp, passed_sp, batch)
                for t in range(NT):
                    sp.dma_start(
                        f32(q_stack[SHIFT_ROW:SHIFT_ROW + 1, h0:h0 + H // 2, t * P:(t + 1) * P]),
                        f32(shift_T[half][t * (H // 2):(t + 1) * (H // 2), :]),
                    ).then_inc(s_shift[half], 16)

            def step(l, b, f, n):
                if n is not None:
                    load_x(n)
                    if isinstance(n, int) and n == 0:
                        w_qkv_v = W_qkv.rearrange("(c p) n -> p c n", p=P)
                        for c in range(KC):
                            sp.dma_start(w_qkv_in[:, c], w_qkv_v[:, c]).then_inc(s_wqkv[c], 16)
                        sp.dma_start(gq_bc[:], g_q.partition_broadcast(P)).then_inc(s_gains, 16)
                        sp.dma_start(gk_bc[:], g_k.partition_broadcast(P)).then_inc(s_gains, 16)
                        sp.dma_start(w_out_in[:], W_out.rearrange("(c p) n -> p c n", p=P)).then_inc(s_wout, 16)
                        for k, w in enumerate((L1_Wq, L1_Wk, L1_Wv)):
                            sp.dma_start(w1_in[:, k], w[1].rearrange("(e p) d -> p e d", p=P)).then_inc(s_w1, 16)
                        sp.dma_start(wo1_in[:], L1_Wo.rearrange("(j i) n -> i j n", i=DK)).then_inc(s_wo1, 16)
                if b is not None:
                    wait(sp, v_x1, at(b, 2, 0))
                    settle(sp, passed_sp, b)
                    sp.dma_start(resid[:], x[b].rearrange("(t p) d -> p t d", p=P)).then_inc(s_resid, 16)
                if l is not None:
                    wait(sp, v_k1, at(l, 1, 0))
                    settle(sp, passed_sp, l)
                    wait(sp, g_pad, at(l, 1, 0))
                    settle(sp, passed_sp, l)
                    sp.dma_start(mask_bc[:], cond[l].partition_broadcast(P)).then_inc(s_mask, 16)
                if b is not None:
                    shift_rows(1, b)
                if l is not None:
                    sp.wait_ge(v_x2, at(l, 2, 2))
                    settle(sp, passed_sp, l)
                    sp.dma_start(out[l].rearrange("(t p) d -> p t d", p=P), x1[:]).then_inc(s_out, 16)
                if f is not None:
                    shift_rows(0, f)

            steps(sp, step)
            sp.wait_ge(s_out, 16 * B)

        @block.gpsimd
        def _(pool):
            g = nc.gpsimd
            g.memset(ident[:], 0.0).then_inc(s_const, 1)
            g.memset(minus_half[:], -0.5).then_inc(s_const, 1)
            g.memset(wq1[:], 0.0).then_inc(s_const, 1)
            g.memset(wk1[:], 0.0).then_inc(s_const, 1)
            pool.wait_ge(s_const, 4)
            g.affine_select(out=ident[:], in_=ident[:], compare_op=ALU.not_equal, fill=1.0, base=0,
                            pattern=[[-1, P]], channel_multiplier=1).then_inc(s_ident, 1)
            pool.wait_ge(s_ident, 1)
            g.tensor_copy(ident_r[:], ident[:]).then_inc(s_ident, 1)

            def gains():
                pool.wait_ge(s_gains, 32)
                g.tensor_tensor(gain_bc[:], gq_bc[:], gk_bc[:], ALU.mult).then_inc(s_gain, 1)
                pool.wait_ge(s_gain, 1)
                g.tensor_scalar(gain_bc[:], gain_bc[:], HD ** -0.5, None, ALU.mult).then_inc(s_gain, 1)
                pool.wait_ge(s_gain, 2)

            def layer1_weights():
                pool.wait_ge(s_w1, 48)
                for k in range(3):
                    g.tensor_copy(wq1[:, :, 32 * k:32 * k + DK], w1_in[:, 0]).then_inc(s_w1sb, 1)
                    g.tensor_copy(wk1[:, :, 32 * k:32 * k + DK], w1_in[:, 1]).then_inc(s_w1sb, 1)
                g.tensor_copy(wq1[:, :, 96:96 + DK], w1_in[:, 2]).then_inc(s_w1sb, 1)

            def x_norm(n):
                wait(pool, a_xnT, at(n, 4, 0))
                pool.wait_ge(s_mod, 2)
                settle(pool, passed_pool, n)
                g.tensor_copy(mod_cur[:], mod_all[:, n]).then_inc(g_mod, 1)
                pool.wait_ge(a_xms, at(n, 2, 2))
                settle(pool, passed_pool, n)
                g.tensor_scalar(x_ms[:], x_ms[:], EPS, None, ALU.add).then_inc(g_xeps, 1)
                pool.wait_ge(g_xeps, at(n, 1, 1))
                settle(pool, passed_pool, n)
                g.tensor_tensor(x_rstd[:], x_ms[:], minus_half[:, 0:NT], ALU.pow).then_inc(g_xrstd, 1)

            def x_split(n):
                pool.wait_ge(a_xnT, at(n, 4, 4))
                if not isinstance(n, int) or n > 0:
                    pool.wait_ge(p_v, at(n, 2, 0))
                settle(pool, passed_pool, n)
                g.tensor_copy(xn_hi[:], xn_T[:]).then_inc(g_xhi, 1)
                pool.wait_ge(g_xhi, at(n, 1, 1))
                settle(pool, passed_pool, n)
                g.tensor_tensor(xn_lo[:], xn_T[:], f32(xn_hi[:]), ALU.subtract).then_inc(g_xlo, 1)

            def rstd(f, j):
                pool.wait_ge(v_ms, at(f, 4, j + 1))
                settle(pool, passed_pool, f)
                g.tensor_scalar(head_ms[:, j], head_ms[:, j], EPS, None, ALU.add).then_inc(g_keps, 1)
                pool.wait_ge(g_keps, at(f, 4, j + 1))
                settle(pool, passed_pool, f)
                g.tensor_tensor(head_rstd[:, j], head_ms[:, j], minus_half[:], ALU.pow).then_inc(g_rstd, 1)

            def k_gain(f, t):
                pool.wait_ge(a_raw, at(f, 4, 2 * t + 2))
                k = qk_raw[:, t, 1].rearrange("p (h d) -> p h d", d=HD)
                gain = gain_bc[:].unsqueeze(1).to_broadcast([P, H, HD])
                g.tensor_tensor(k, k, gain, ALU.mult).then_inc(g_kgain, 1)

            def split(f, j):
                t, k = j // 2, j % 2
                dst = qk_split[:, k, t]
                val = qk_raw[:, t, k].rearrange("p (h d) -> p h d", d=HD)
                lo, again = (1, 2) if k == 0 else (2, 1)
                pool.wait_ge(a_hi, at(f, 4, j + 1))
                settle(pool, passed_pool, f)
                g.tensor_tensor(dst[:, :, lo * HD:(lo + 1) * HD], val, f32(dst[:, :, 0:HD]),
                                ALU.subtract).then_inc(g_split, 1)
                g.tensor_copy(dst[:, :, again * HD:(again + 1) * HD], f32(dst[:, :, 0:HD])).then_inc(g_split, 1)

            def step(l, b, f, n):
                if f is not None and isinstance(f, int) and f == 0:
                    gains()
                if l is not None:
                    pool.wait_ge(s_mask, at(l, 16, 16))
                    wait(pool, v_score1, at(l, 4, 0))
                    settle(pool, passed_pool, l)
                    g.tensor_scalar(pad_bias[:], mask_bc[:], -1.0, 1.0, ALU.mult, ALU.add).then_inc(g_pad0, 1)
                    pool.wait_ge(g_pad0, at(l, 1, 1))
                    settle(pool, passed_pool, l)
                    g.tensor_scalar(pad_bias[:], pad_bias[:], NEG, None, ALU.mult).then_inc(g_pad, 1)
                    wait(pool, v_row1, at(l, 4, 0))
                    settle(pool, passed_pool, l)
                    g.tensor_copy(vmask[:], cond_T[:, l]).then_inc(g_vmask, 1)
                if f is not None:
                    rstd(f, 0)
                    k_gain(f, 0)
                    rstd(f, 1)
                    split(f, 0)
                    rstd(f, 2)
                    k_gain(f, 1)
                    split(f, 1)
                    rstd(f, 3)
                if l is not None:
                    pool.wait_ge(v_k1, at(l, 1, 1))
                    settle(pool, passed_pool, l)
                    g.tensor_copy(k1[:], kv1[0:96]).then_inc(g_k1hi, 1)
                    pool.wait_ge(g_k1hi, at(l, 1, 1))
                    settle(pool, passed_pool, l)
                    g.tensor_tensor(k1[64:96], kv1[64:96], f32(k1[64:96]), ALU.subtract).then_inc(g_k1lo, 1)
                    pool.wait_ge(g_k1lo, at(l, 1, 1))
                if f is not None:
                    split(f, 2)
                    split(f, 3)
                if n is not None:
                    x_norm(n)
                if b is not None:
                    pool.wait_ge(v_o, at(b, NG, NG))
                    pool.wait_ge(s_resid, at(b, 16, 16))
                    settle(pool, passed_pool, b)
                    g.tensor_tensor(resid[:], resid[:], o_sb[:], ALU.add).then_inc(g_resid, 1)
                if n is not None:
                    x_split(n)
                if f is not None and isinstance(f, int) and f == 0:
                    layer1_weights()

            steps(pool, step)

        @block.scalar
        def _(act):
            a = nc.scalar
            for c in range(KC):
                act.wait_ge(s_wqkv[c], 16)
                a.activation(wqkv_hi[:, c], w_qkv_in[:, c], ACT.Copy).then_inc(s_whi, 1)
                if c == 1:
                    pass
            act.wait_ge(s_wout, 16)
            a.activation(wout_hi[:], w_out_in[:], ACT.Copy).then_inc(s_whi, 1)

            def x_squares(n):
                act.wait_ge(s_x, at(n, 16, 16))
                wait(act, v_x, at(n, 2, 0))
                for t in range(NT):
                    a.activation(xn_T[:, 2 * t:2 * t + 2].rearrange("p c n -> p (c n)"), x_in[:, t], ACT.Square,
                                 scale=D ** -0.5, accum_out=x_ms[:, t:t + 1]).then_inc(a_xms, 1)

            def modulate(n):
                act.wait_ge(g_mod, at(n, 1, 1))
                wait(act, g_xlo, at(n, 1, 0))
                for c in range(KC):
                    act.wait_ge(p_xT, at(n, 2, c // 2 + 1))
                    a.activation(xn_T[:, c], ps_w[c // 2][:, (c % 2) * N:(c % 2 + 1) * N], ACT.Identity,
                                 scale=mod_cur[:, c:c + 1], bias=mod_cur[:, KC + c:KC + c + 1]).then_inc(a_xnT, 1)

            def qk_out(f, j):
                t, k = j // 2, j % 2
                act.wait_ge(p_qkv, at(f, 4, j + 1))
                wait(act, g_split, at(f, 8, 0))
                a.activation(qk_raw[:, t, k], ps_w[j % 2][:], ACT.Copy).then_inc(a_raw, 1)
                wait(act, v_ms, at(f, 4, j - 1) if j >= 2 else at(f, 4, 0))
                a.activation(squares[:, j % 2], ps_w[j % 2][:], ACT.Square, scale=HD ** -0.5).then_inc(a_sq, 1)

            def qk_hi(f, j):
                t, k = j // 2, j % 2
                act.wait_ge(v_qkn, at(f, 4, j + 1))
                wait(act, p_stack, at(f, 4 * NG, 0))
                a.activation(qk_split[:, k, t, :, 0:HD], qk_raw[:, t, k].rearrange("p (h d) -> p h d", d=HD),
                             ACT.Copy).then_inc(a_hi, 1)

            def stack_out(f, j):
                k, t = j // 2, j % 2
                dst = (q_stack, k_stack)[k]
                act.wait_ge(p_stack, at(f, 4 * NG, 4 * (NG - 1) + j + 1))
                a.activation(dst[0:SHIFT_ROW, (NG - 1) * G:, t * P:(t + 1) * P],
                             ps_w[j % 2][0:SHIFT_ROW, :].rearrange("p (h n) -> p h n", h=G),
                             ACT.Copy).then_inc(a_stack, 1)

            def v_out(f, t):
                act.wait_ge(p_v, at(f, 2, t + 1))
                wait(act, p_o, at(f, H, 0))
                a.activation(v_one[:, t, :, 0:HD], ps_w[0][:].rearrange("p (h d) -> p h d", d=HD),
                             ACT.Copy).then_inc(a_v, 1)

            def exp(b, h):
                act.wait_ge(p_logit, at(b, H, h + 1))
                wait(act, p_o, at(b, H, h - 2) if h >= 3 else at(b, H, 0))
                a.activation(e[h % 3][:].rearrange("p t n -> p (t n)"), ps_logit[h % 2][:],
                             ACT.Exp).then_inc(a_e, 1)

            def o_T_hi(b, t):
                act.wait_ge(p_oT, at(b, 2, t + 1))
                wait(act, p_wout, at(b, 2, 0))
                a.activation(o_hi[:, :, t * P:(t + 1) * P], ps_w[1][:].rearrange("p (c n) -> p c n", c=KC),
                             ACT.Copy).then_inc(a_ohi, 1)

            def q1_out(l):
                act.wait_ge(p_proj1, at(l, 2, 1))
                wait(act, p_score1, at(l, 4, 0))
                a.activation(q1[:], ps_w[1][0:96, :], ACT.Copy, scale=-(DK ** -0.5)).then_inc(a_q1, 1)
                wait(act, p_vT, at(l, 1, 0))
                a.activation(kv1[96:112], ps_w[1][96:112, :], ACT.Copy).then_inc(a_vT, 1)

            def v1_out(l):
                act.wait_ge(p_vT, at(l, 1, 1))
                wait(act, p_o1, at(l, 4, 0))
                a.activation(v1[:].rearrange("p t d -> p (t d)"), ps_w[1][:, 0:QT * DK], ACT.Copy).then_inc(a_v1, 1)

            def exp1(l, q):
                act.wait_ge(v_score1, at(l, 4, q + 1))
                a.activation(e1[q % 2][:], e1[q % 2][:], ACT.Exp, scale=-1.0, bias=min1[:, q:q + 1],
                             accum_out=sum1[:, q:q + 1]).then_inc(a_e1, 1)

            def e1_T_out(l, q):
                act.wait_ge(p_eT, at(l, 4, q + 1))
                wait(act, p_o1, at(l, 4, q - 1) if q >= 2 else at(l, 4, 0))
                a.activation(e1_T[q % 2][:].rearrange("p t n -> p (t n)"), ps_w[1][:], ACT.Copy).then_inc(a_eT, 1)

            def head1_T_out(l):
                act.wait_ge(p_headT, at(l, 1, 1))
                wait(act, p_out1, at(l, 2, 0))
                a.activation(head1_T[:], ps_w[1][0:DK, :], ACT.Copy).then_inc(a_headT, 1)

            def step(l, b, f, n):
                if f is not None:
                    qk_out(f, 0)
                if l is not None:
                    q1_out(l)
                if f is not None:
                    qk_out(f, 1)
                    qk_hi(f, 0)
                    qk_out(f, 2)
                    qk_hi(f, 1)
                    qk_out(f, 3)
                    qk_hi(f, 2)
                if f is not None and b is None:
                    qk_hi(f, 3)
                for h in range(H):
                    if b is not None:
                        exp(b, h)
                        if h == 0 and f is not None:
                            qk_hi(f, 3)
                    if l is not None:
                        if h == 1:
                            v1_out(l)
                        if h in (2, 3, 7, 9):
                            exp1(l, (2, 3, 7, 9).index(h))
                        if h in (4, 5, 10, 11):
                            e1_T_out(l, (4, 5, 10, 11).index(h))
                        if h == 14:
                            head1_T_out(l)
                    if n is not None and h == 12:
                        x_squares(n)
                if f is not None:
                    v_out(f, 0)
                    stack_out(f, 0)
                    stack_out(f, 1)
                if b is not None:
                    o_T_hi(b, 0)
                if f is not None:
                    v_out(f, 1)
                if b is not None:
                    o_T_hi(b, 1)
                if f is not None:
                    stack_out(f, 2)
                    stack_out(f, 3)
                if n is not None:
                    modulate(n)

            steps(act, step)

        @block.vector
        def _(dve):
            v = nc.vector
            v.memset(v_one[:, :, :, HD:HD + 1], 1.0).then_inc(s_ones, 1)
            dve.wait_ge(s_condT, 1)
            v.tensor_copy(cond_T[:].rearrange("p b c -> p c b"),
                          ps_w[0][:, 0:KC * B].rearrange("p (c b) -> p c b", b=B)).then_inc(s_condT_sb, 1)
            v.tensor_copy(biasgain_T[:], ps_w[0][:, 64:76]).then_inc(s_condT_sb, 1)
            dve.wait_ge(s_condT_sb, 2)
            dve.wait_ge(s_mod_ps, 1)
            v.tensor_tensor(mod_all[:].rearrange("p b c -> p c b"),
                            ps_w[1][:, 0:2 * KC * B].rearrange("p (c b) -> p c b", b=B),
                            biasgain_T[:, 0:8].unsqueeze(2).to_broadcast([P, 8, B]), ALU.add).then_inc(s_mod_b, 1)
            dve.wait_ge(s_mod_b, 1)
            v.tensor_scalar(mod_all[:, :, 0:KC], mod_all[:, :, 0:KC], 1.0, None, ALU.add).then_inc(s_mod, 1)
            dve.wait_ge(s_mod, 1)
            v.tensor_tensor(mod_all[:, :, 0:KC], mod_all[:, :, 0:KC],
                            biasgain_T[:, 8:12].unsqueeze(1).to_broadcast([P, B, KC]), ALU.mult).then_inc(s_mod, 1)

            def weights():
                for c in range(KC):
                    dve.wait_ge(s_whi, c + 1)
                    v.tensor_tensor(wqkv_lo[:, c], w_qkv_in[:, c], f32(wqkv_hi[:, c]),
                                    ALU.subtract).then_inc(s_wsplit, 1)
                dve.wait_ge(s_whi, KC + 1)
                v.tensor_tensor(wout_lo[:], w_out_in[:], f32(wout_hi[:]), ALU.subtract).then_inc(s_wsplit, 1)
                dve.wait_ge(s_wo1, 16)
                v.tensor_reduce(wo1[:], wo1_in[:].rearrange("i j n -> i n j"), AX.X, ALU.add).then_inc(s_wo1sb, 1)
                dve.wait_ge(s_wsplit, KC + 1)
                dve.wait_ge(s_wo1sb, 1)
                v.memset(f32(k_stack[SHIFT_ROW:SHIFT_ROW + 1, :, :]), 1.0).then_inc(s_ones, 1)

            def x_normalise(n):
                dve.wait_ge(g_xrstd, at(n, 1, 1))
                for t in range(NT):
                    v.tensor_scalar(x_in[:, t], x_in[:, t], x_rstd[:, t:t + 1], None, ALU.mult).then_inc(v_x, 1)

            def mean_squares(f, j):
                dve.wait_ge(a_sq, at(f, 4, j + 1))
                v.tensor_reduce(head_ms[:, j], squares[:, j % 2].rearrange("p (h d) -> p h d", d=HD),
                                AX.X, ALU.add).then_inc(v_ms, 1)

            def qk_norm(f, j):
                t, k = j // 2, j % 2
                dve.wait_ge(g_rstd, at(f, 4, j + 1))
                dve.wait_ge(a_raw, at(f, 4, j + 1))
                if k == 1:
                    dve.wait_ge(g_kgain, at(f, 2, t + 1))
                val = qk_raw[:, t, k].rearrange("p (h d) -> p h d", d=HD)
                v.tensor_tensor(val, val, head_rstd[:, j].unsqueeze(2).to_broadcast([P, H, HD]),
                                ALU.mult).then_inc(v_qkn, 1)

            def stack_out(f, j):
                grp, k, t = j // 4, j // 2 % 2, j % 2
                dst = (q_stack, k_stack)[k]
                dve.wait_ge(p_stack, at(f, 4 * NG, j + 1))
                v.tensor_copy(dst[0:SHIFT_ROW, grp * G:(grp + 1) * G, t * P:(t + 1) * P],
                              ps_w[0][0:SHIFT_ROW, :].rearrange("p (h n) -> p h n", h=G)).then_inc(v_stack, 1)

            def row_max(b, h):
                dve.wait_ge(p_max, at(b, H, h + 1))
                v.tensor_reduce(maxima[:, h // 8, :, h % 8], ps_max[h % 2][:].rearrange("p (t n) -> p t n", t=NT),
                                AX.X, ALU.max).then_inc(v_max, 1)

            def shift_out(batch, half):
                dve.wait_ge(p_maxT, at(batch, 2, half + 1))
                wait(dve, s_shift[half], at(batch, 32, 0))
                v.tensor_scalar(shift_T[half][:], ps_w[1][0:H, 0:P], -1.0, None, ALU.mult).then_inc(v_shift, 1)

            def o_norm(b, grp):
                dve.wait_ge(p_o, at(b, H, G * (grp + 1)))
                if grp == 0:
                    wait(dve, p_oT, at(b, 2, 0))
                    wait(dve, g_resid, at(b, 1, 0))
                o = ps_o[grp % 2][:, 0:NT * G * (HD + 1)].rearrange("p (t h d) -> p t h d", t=NT, h=G)
                v.reciprocal(o_rden[:], o[:, :, :, HD]).then_inc(v_rden, 1)
                dve.wait_ge(v_rden, at(b, NG, grp + 1))
                for t in range(NT):
                    ins = v.tensor_tensor(
                        o_sb[:, t, grp * G * HD:(grp + 1) * G * HD].rearrange("p (h d) -> p h d", d=HD),
                        o[:, t, :, 0:HD], o_rden[:, t].unsqueeze(2).to_broadcast([P, G, HD]), ALU.mult)
                ins.then_inc(v_o, 1)

            def o_T_lo(b, t):
                dve.wait_ge(a_ohi, at(b, 2, t + 1))
                v.tensor_tensor(o_lo[:, :, t * P:(t + 1) * P], ps_w[1][:].rearrange("p (c n) -> p c n", c=KC),
                                f32(o_hi[:, :, t * P:(t + 1) * P]), ALU.subtract).then_inc(v_olo, 1)

            def x1_out(b, t):
                dve.wait_ge(p_wout, at(b, 2, t + 1))
                dve.wait_ge(g_resid, at(b, 1, 1))
                wait(dve, s_out, at(b, 16, 0))
                v.tensor_tensor(x1[:, t], ps_w[0][:], resid[:, t], ALU.add).then_inc(v_x1, 1)

            def q1_lo(l):
                dve.wait_ge(a_q1, at(l, 1, 1))
                dve.wait_ge(a_vT, at(l, 1, 1))
                v.scalar_tensor_tensor(out=q1[32:64], in0=ps_w[1][32:64, :], scalar=-(DK ** -0.5),
                                       in1=f32(q1[32:64]), op0=ALU.mult, op1=ALU.subtract).then_inc(v_q1, 1)

            def k1_mask(l):
                dve.wait_ge(p_proj1, at(l, 2, 2))
                dve.wait_ge(s_mask, at(l, 16, 16))
                wait(dve, g_k1lo, at(l, 1, 0))
                v.tensor_tensor(kv1[0:96], ps_w[1][0:96, :], mask_bc[0:96, :], ALU.mult).then_inc(v_k1, 1)

            def score1(l, q):
                dve.wait_ge(p_score1, at(l, 4, q + 1))
                dve.wait_ge(g_pad, at(l, 1, 1))
                wait(dve, p_eT, at(l, 4, q - 1) if q >= 2 else at(l, 4, 0))
                settle(dve, passed_dve, l)
                v.tensor_tensor_reduce(out=e1[q % 2][:], in0=ps_w[1][:], in1=pad_bias[:], scale=1.0, scalar=3e38,
                                       op0=ALU.add, op1=ALU.min, accum_out=min1[:, q:q + 1]).then_inc(v_score1, 1)

            def row_scale1(l, q):
                dve.wait_ge(a_e1, at(l, 4, q + 1))
                dve.wait_ge(g_vmask, at(l, 1, 1))
                v.reciprocal(row1[:, q:q + 1], sum1[:, q:q + 1]).then_inc(v_rsum1, 1)
                dve.wait_ge(v_rsum1, at(l, 4, q + 1))
                v.tensor_tensor(row1[:, q:q + 1], row1[:, q:q + 1], vmask[:, q:q + 1], ALU.mult).then_inc(v_row1, 1)

            def head1_out(l, q):
                dve.wait_ge(p_o1, at(l, 4, q + 1))
                dve.wait_ge(v_row1, at(l, 4, q + 1))
                wait(dve, p_headT, at(l, 1, 0))
                v.tensor_scalar(head1[:, q], ps_w[1][:, 0:DK], row1[:, q:q + 1], None, ALU.mult).then_inc(v_head1, 1)

            def x2_out(l, t):
                dve.wait_ge(p_out1, at(l, 2, t + 1))
                v.tensor_tensor(x1[:, t], ps_w[1][:], x1[:, t], ALU.add).then_inc(v_x2, 1)

            def step(l, b, f, n):
                if f is not None and isinstance(f, int) and f == 0:
                    weights()
                if f is not None:
                    mean_squares(f, 0)
                if l is not None:
                    q1_lo(l)
                if b is not None:
                    row_max(b, 8)
                    row_max(b, 9)
                if f is not None:
                    qk_norm(f, 0)
                    mean_squares(f, 1)
                if l is not None:
                    k1_mask(l)
                if b is not None:
                    row_max(b, 10)
                    row_max(b, 11)
                if f is not None:
                    qk_norm(f, 1)
                    mean_squares(f, 2)
                if b is not None:
                    row_max(b, 12)
                    row_max(b, 13)
                if f is not None:
                    qk_norm(f, 2)
                    mean_squares(f, 3)
                if b is not None:
                    row_max(b, 14)
                    row_max(b, 15)
                    shift_out(b, 1)
                if f is not None:
                    qk_norm(f, 3)
                for h in range(H):
                    if f is not None and h >= 4:
                        stack_out(f, h - 4)
                    if b is not None and h in (5, 9, 13):
                        o_norm(b, h // 4 - 1)
                    if l is not None:
                        if h in (1, 2, 6, 8):
                            score1(l, (1, 2, 6, 8).index(h))
                        if h in (4, 5, 8, 11):
                            row_scale1(l, (4, 5, 8, 11).index(h))
                        if h in (5, 7, 11, 12):
                            head1_out(l, (5, 7, 11, 12).index(h))
                        if h in (14, 15):
                            x2_out(l, h - 14)
                    if f is not None and h >= 8:
                        row_max(f, h - 8)
                    if n is not None and h == 14:
                        x_normalise(n)
                if b is not None:
                    o_norm(b, 3)
                    o_T_lo(b, 0)
                    o_T_lo(b, 1)
                    x1_out(b, 0)
                if f is not None:
                    shift_out(f, 0)
                if b is not None:
                    x1_out(b, 1)

            steps(dve, step)

        @block.tensor
        def _(pe):
            mm, tr = nc.tensor.matmul, nc.tensor.transpose
            pe.wait_ge(s_ident, 2)
            pe.wait_ge(s_cond, 16)
            pe.wait_ge(s_rows, 32)
            for c in range(KC):
                tr(ps_w[0][:, c * B:(c + 1) * B], cond_in[:, c * P:(c + 1) * P], ident[0:B, 0:B])
            tr(ps_w[0][:, 64:76], rows_in[0:12, :], ident[0:12, 0:12]).then_inc(s_condT, 1)
            pe.wait_ge(s_condT_sb, 2)
            pe.wait_ge(s_wemb, 16 * KC)
            for m in range(2 * KC):
                for c in range(KC):
                    ins = mm(ps_w[1][:, m * B:(m + 1) * B], w_emb_in[:, c, m * P:(m + 1) * P], cond_T[:, :, c],
                             start=(c == 0), stop=(c == KC - 1))
            ins.then_inc(s_mod_ps, 1)

            freed = [None, None]

            def use(k, reader, value):
                if freed[k] is not None:
                    wait(pe, *freed[k])
                freed[k] = (reader, value)
                return ps_w[k]

            def product3(ps, a_hi_, a_lo_, w_hi_, w_lo_, toks, cols):
                todo = [(a, w, c) for c in range(KC) for a, w in ((a_hi_, w_hi_), (a_lo_, w_hi_), (a_hi_, w_lo_))]
                for n, (a, w, c) in enumerate(todo):
                    ins = mm(ps[:], a[:, c, toks], w[:, c, cols], start=(n == 0), stop=(n == len(todo) - 1))
                return ins

            def x_T(n, j):
                ps = use(j, a_xnT, at(n, 4, 2 * j + 2))
                pe.wait_ge(v_x, at(n, 2, 2))
                for c in range(2):
                    for t in range(NT):
                        ins = tr(ps[:, c * N + t * P:c * N + (t + 1) * P],
                                 x_in[:, t, (2 * j + c) * P:(2 * j + c + 1) * P], ident[:])
                ins.then_inc(p_xT, 1)

            def qk_product(f, j):
                t, k = j // 2, j % 2
                ps = use(j % 2, a_sq, at(f, 4, j + 1))
                pe.wait_ge(g_xlo, at(f, 1, 1))
                product3(ps, xn_hi, xn_lo, wqkv_hi, wqkv_lo, slice(t * P, (t + 1) * P),
                         slice(k * D, (k + 1) * D)).then_inc(p_qkv, 1)

            def v_product(f, t):
                ps = use(0, a_v, at(f, 2, t + 1))
                product3(ps, xn_hi, xn_lo, wqkv_hi, wqkv_lo, slice(t * P, (t + 1) * P),
                         slice(2 * D, 3 * D)).then_inc(p_v, 1)

            def stack(f, j):
                grp, k, t = j // 4, j // 2 % 2, j % 2
                if grp < NG - 1:
                    ps = use(0, v_stack, at(f, 12, j + 1))
                else:
                    ps = use(j % 2, a_stack, at(f, 4, j - 4 * (NG - 1) + 1))
                pe.wait_ge(g_split, at(f, 8, 2 * (2 * t + k) + 2))
                for h in range(G):
                    ins = tr(ps[0:SHIFT_ROW, h * P:(h + 1) * P].bitcast(F32R), qk_split[:, k, t, grp * G + h, :],
                             ident_r[:])
                ins.then_inc(p_stack, 1)

            def max_logits(b, h):
                wait(pe, v_max, at(b, H, h - 1))
                if h < (NG - 1) * G:
                    pe.wait_ge(v_stack, at(b, 12, 4 * (h // G + 1)))
                else:
                    pe.wait_ge(a_stack, at(b, 4, 4))
                for t in range(NT):
                    ins = mm(ps_max[h % 2][:, t * N:(t + 1) * N], q_stack[0:SHIFT_ROW, h, t * P:(t + 1) * P],
                             k_stack[0:SHIFT_ROW, h, :], start=True, stop=True)
                ins.then_inc(p_max, 1)

            def max_T(batch, half):
                ps = use(1, v_shift, at(batch, 2, half + 1))
                pe.wait_ge(v_max, at(batch, H, (half + 1) * (H // 2)))
                tr(ps[0:H, 0:P], maxima[:, half].rearrange("p t h -> p (t h)"), ident[:]).then_inc(p_maxT, 1)

            def logits(b, h):
                wait(pe, a_e, at(b, H, h - 1))
                pe.wait_ge(s_shift[h // 8], at(b, 32, 32))
                for t in range(NT):
                    ins = mm(ps_logit[h % 2][:, t * N:(t + 1) * N], k_stack[:, h, t * P:(t + 1) * P],
                             q_stack[:, h, :], start=True, stop=True)
                ins.then_inc(p_logit, 1)

            def weighted_v(b, h):
                grp, hh = h // G, h % G
                if hh == 0:
                    wait(pe, v_o, at(b, NG, grp - 1))
                pe.wait_ge(a_e, at(b, H, h + 1))
                pe.wait_ge(a_v, at(b, 2, 2))
                for q in range(NT):
                    for t in range(NT):
                        o0 = (q * G + hh) * (HD + 1)
                        ins = mm(ps_o[grp % 2][:, o0:o0 + HD + 1], e[h % 3][:, t, q * P:(q + 1) * P],
                                 v_one[:, t, h, :], start=(t == 0), stop=(t == NT - 1))
                ins.then_inc(p_o, 1)

            def o_T(b, t):
                ps = use(1, v_olo, at(b, 2, t + 1))
                pe.wait_ge(v_o, at(b, NG, NG))
                for c in range(KC):
                    ins = tr(ps[:, c * P:(c + 1) * P], o_sb[:, t, c * P:(c + 1) * P], ident[:])
                ins.then_inc(p_oT, 1)

            def out_product(b, t):
                ps = use(0, v_x1, at(b, 2, t + 1))
                pe.wait_ge(v_olo, at(b, 2, t + 1))
                product3(ps, o_hi, o_lo, wout_hi, wout_lo, slice(t * P, (t + 1) * P),
                         slice(0, D)).then_inc(p_wout, 1)

            def project1(l, k):
                w, m = ((wq1, 112), (wk1, 96))[k]
                ps = use(1, (v_q1, v_k1)[k], at(l, 1, 1))
                pe.wait_ge(v_x1, at(l, 2, 2))
                for t in range(ET):
                    ins = mm(ps[0:m, :], w[:, t, :], x1[:, t, :], start=(t == 0), stop=(t == ET - 1))
                ins.then_inc(p_proj1, 1)

            def v1_T(l):
                ps = use(1, a_v1, at(l, 1, 1))
                pe.wait_ge(a_vT, at(l, 1, 1))
                settle(pe, passed_pe, l)
                for t in range(QT):
                    ins = tr(ps[:, t * DK:(t + 1) * DK], kv1[96:112, t * P:(t + 1) * P], ident[96:112, 96:112])
                ins.then_inc(p_vT, 1)

            def scores1(l, q):
                ps = use(1, v_score1, at(l, 4, q + 1))
                pe.wait_ge(v_q1, at(l, 1, 1))
                pe.wait_ge(g_k1lo, at(l, 1, 1))
                mm(ps[:], q1[:, q * P:(q + 1) * P], k1[:], start=True, stop=True).then_inc(p_score1, 1)

            def e1_transposes(l, q):
                ps = use(1, a_eT, at(l, 4, q + 1))
                pe.wait_ge(a_e1, at(l, 4, q + 1))
                for t in range(QT):
                    ins = tr(ps[:, t * P:(t + 1) * P], e1[q % 2][:, t * P:(t + 1) * P], ident[:])
                ins.then_inc(p_eT, 1)

            def weighted_v1(l, q):
                ps = use(1, v_head1, at(l, 4, q + 1))
                pe.wait_ge(a_eT, at(l, 4, q + 1))
                pe.wait_ge(a_v1, at(l, 1, 1))
                for t in range(QT):
                    ins = mm(ps[:, 0:DK], e1_T[q % 2][:, t, :], v1[:, t, :], start=(t == 0), stop=(t == QT - 1))
                ins.then_inc(p_o1, 1)

            def head1_transposes(l):
                ps = use(1, a_headT, at(l, 1, 1))
                pe.wait_ge(v_head1, at(l, 4, 4))
                for q in range(QT):
                    ins = tr(ps[0:DK, q * P:(q + 1) * P], head1[:, q, :], ident[:])
                ins.then_inc(p_headT, 1)

            def out1(l, t):
                ps = use(1, v_x2, at(l, 2, t + 1))
                pe.wait_ge(a_headT, at(l, 1, 1))
                mm(ps[:], wo1[:, t * P:(t + 1) * P], head1_T[:], start=True, stop=True).then_inc(p_out1, 1)

            layer1 = [(v1_T, None), (scores1, 0), (scores1, 1), (e1_transposes, 0), (e1_transposes, 1),
                      (weighted_v1, 0), (scores1, 2), (weighted_v1, 1), (scores1, 3), (e1_transposes, 2),
                      (e1_transposes, 3), (weighted_v1, 2), (weighted_v1, 3), (head1_transposes, None),
                      (out1, 0), (out1, 1)]

            def step(l, b, f, n):
                if f is not None:
                    freed[:] = [(a_xnT, at(f, 4, 2)), (a_xnT, at(f, 4, 4))]
                    if isinstance(f, int) and f == 0:
                        pe.wait_ge(s_wsplit, KC)
                        pe.wait_ge(s_ones, 2)
                    qk_product(f, 0)
                if l is not None:
                    if isinstance(l, int) and l == 0:
                        pe.wait_ge(s_w1sb, 7)
                        pe.wait_ge(s_wo1sb, 1)
                    project1(l, 0)
                if b is not None:
                    max_logits(b, 8)
                    max_logits(b, 9)
                if f is not None:
                    qk_product(f, 1)
                if l is not None:
                    project1(l, 1)
                if b is not None:
                    max_logits(b, 10)
                    max_logits(b, 11)
                if f is not None:
                    qk_product(f, 2)
                if b is not None:
                    max_logits(b, 12)
                    max_logits(b, 13)
                if f is not None:
                    qk_product(f, 3)
                if b is not None:
                    max_logits(b, 14)
                    max_logits(b, 15)
                    max_T(b, 1)
                for h in range(H):
                    if b is not None:
                        logits(b, h)
                        if h >= 1:
                            weighted_v(b, h - 1)
                    if f is not None and h >= 4:
                        stack(f, h - 4)
                    if l is not None:
                        job, q = layer1[h]
                        job(l) if q is None else job(l, q)
                    if f is not None and h >= 8:
                        max_logits(f, h - 8)
                if b is not None:
                    weighted_v(b, H - 1)
                if f is not None:
                    v_product(f, 0)
                    stack(f, 12)
                    stack(f, 13)
                if b is not None:
                    o_T(b, 0)
                if f is not None:
                    v_product(f, 1)
                if b is not None:
                    o_T(b, 1)
                if f is not None:
                    stack(f, 14)
                    stack(f, 15)
                if b is not None:
                    if isinstance(b, int) and b == 0:
                        pe.wait_ge(s_wsplit, KC + 1)
                    out_product(b, 0)
                if f is not None:
                    max_T(f, 0)
                if b is not None:
                    out_product(b, 1)
                if n is not None:
                    x_T(n, 0)
                    x_T(n, 1)

            steps(pe, step)


_INS = ['x', 'cond_2048', 'L0_cond_W_emb', 'L0_cond_b_emb', 'L0_cond_g_norm', 'L0_cond_W_qkv', 'L0_cond_g_q',
        'L0_cond_g_k', 'L0_cond_W_out', 'L1_cond_Wq', 'L1_cond_Wk', 'L1_cond_Wv', 'L1_cond_Wo']
_OUT = ((B, N, D), 'float32')


def kernel(**inputs):
    import numpy as _np
    import concourse.bacc as _bacc
    from concourse import mybir as _mybir
    from concourse.bass_utils import run_bass_kernel_spmd as _run

    nc = _bacc.Bacc("TRN2", target_bir_lowering=False, num_devices=1)
    arrays, args = {}, []
    for name in _INS:
        a = _np.ascontiguousarray(inputs[name])
        arrays[f"in_{name}_dram"] = a
        args.append(nc.dram_tensor(f"in_{name}_dram", a.shape, _mybir.dt.from_np(a.dtype), kind="ExternalInput").ap())
    shape, dtype = _OUT
    args.append(nc.dram_tensor("out_0_dram", shape, _mybir.dt.from_np(_np.dtype(dtype)), kind="ExternalOutput").ap())
    build(nc, *args)
    r = _run(nc, [arrays], core_ids=[0])
    return r.results[0]["out_0_dram"]
```

```python
import concourse.bass as bass
from concourse import mybir
from contextlib import ExitStack


B, N, D, H, HD = 8, 256, 512, 16, 32
P = 128
NT = N // P
KC = D // P
G = 4
NG = H // G
NP = H // 2
S1, DK = 512, 16
ET, QT = N // P, S1 // P
SHIFT_ROW = 3 * HD
PAIR = 7 * HD
ODD = 3 * HD
EPS = 1e-6
NEG = 1e30

QKV_SLOTS = {0: 0, 1: 1, 2: 2, 3: 3, 6: 4, 7: 5}
WOUT_SLOTS = {4: 0, 5: 1}
STACK3_SLOTS = {0: (12, 13), 1: (14, 15)}
STACK_SLOTS = {8: (0, 1), 9: (2, 3), 10: (4, 5), 11: (6, 7), 12: (8, 9), 13: (10, 11)}
MAX3_SLOTS = {2: (12, 13), 3: (14, 15)}
MAX_SLOTS = {10: (0, 1), 11: (2, 3), 12: (4, 5), 13: (6, 7), 14: (8, 9), 15: (10, 11)}
MAX_T_SLOTS = {4: 1, 14: 0}
XT_SLOTS = {11: 0, 12: 1}
PROJ1_SLOTS = {6: 0, 7: 1}
SCORE1_SLOTS = {8: 0, 9: 1, 10: 2, 11: 3}
E1T_SLOTS = {10: 0, 11: 1, 12: 2, 13: 3}
PV1_SLOTS = {11: 0, 12: 1, 13: 2, 14: 3}
NORM_SLOTS = {1: 0, 2: 1, 3: 2, 4: 3}
HI_SLOTS = {2: 0, 3: 1, 4: 2, 5: 3}

F32 = mybir.dt.float32
F32R = mybir.dt.float32r
ACT = mybir.ActivationFunctionType
ALU = mybir.AluOpType
AX = mybir.AxisListType


def at(batch, per_batch, more):
    return batch * per_batch + more


def wait(eng, sem, value):
    if not isinstance(value, int) or value > 0:
        eng.wait_ge(sem, value)


def settle(eng, count, batch):
    if not isinstance(batch, int):
        eng.sem_inc(count, 1)


def f32(ap):
    return ap.bitcast(F32)


def build(nc, x, cond, W_emb, b_emb, g_norm, W_qkv, g_q, g_k, W_out, L1_Wq, L1_Wk, L1_Wv, L1_Wo, out):
    ctx = ExitStack()
    with ctx:
        def sb(name, shape, dt=F32, where=ctx):
            return where.enter_context(nc.sbuf_tensor(name, shape, dt))

        def sem(name):
            return ctx.enter_context(nc.semaphore(name))

        wqkv_hi = sb("wqkv_hi", [P, KC, 3 * D], F32R)
        wqkv_lo = sb("wqkv_lo", [P, KC, 3 * D], F32R)
        wout_hi = sb("wout_hi", [P, KC, D], F32R)
        wout_lo = sb("wout_lo", [P, KC, D], F32R)
        ident_r = sb("ident_r", [P, P], F32R)
        ident = ident_r[:].bitcast(F32)
        gain_bc = sb("gain_bc", [P, HD])
        eps_col = sb("eps_col", [P, 1])
        cond_T = sb("cond_T", [P, B, KC])
        biasgain_T = sb("biasgain_T", [P, 12])
        mod_all = sb("mod_all", [P, B, 2 * KC])
        mod_cur = sb("mod_cur", [P, 2 * KC])
        wq1 = sb("wq1", [P, ET, 112])
        wk1 = sb("wk1", [P, ET, 96])
        wo1 = sb("wo1", [2 * DK, N])[:]

        staging = ExitStack()
        wo1_in = sb("wo1_in", [2 * DK, H, N], F32, staging)
        w1_in = sb("w1_in", [P, 3, ET, DK], F32, staging)
        gq_bc = sb("gq_bc", [P, HD], F32, staging)
        gk_bc = sb("gk_bc", [P, HD], F32, staging)
        w_out_in = sb("w_out_in", [P, KC, D], F32, staging)
        w_emb_in = sb("w_emb_in", [P, KC, 2 * D], F32, staging)
        w_qkv_in = sb("w_qkv_in", [P, KC, 3 * D], F32, staging)
        rows_in = sb("rows_in", [12, P], F32, staging)
        cond_in = sb("cond_in", [B, D], F32, staging)
        staging.close()

        qk_split = sb("qk_split", [P, 2, NT, H, 3 * HD], F32R)
        q_stack = sb("q_stack", [SHIFT_ROW + 1, H, N], F32R)
        k_stack = sb("k_stack", [SHIFT_ROW + 1, H, N], F32R)
        qk_raw = sb("qk_raw", [P, NT, 2, D])
        o_hi = sb("o_hi", [P, NG, N], F32R)
        o_lo = sb("o_lo", [P, NG, N], F32R)
        v_raw = sb("v_raw", [P, NT, D])
        squares = v_raw[:, 0]
        e = [sb(f"e{k}", [P, NT, N]) for k in range(2)]
        head_ms = sb("head_ms", [P, 4, H])
        head_y = sb("head_y", [P, 4, H])
        head_t = sb("head_t", [P, H])
        x_in = sb("x_in", [P, NT, D])
        x_ms = sb("x_ms", [P, NT])
        x_y = sb("x_y", [P, NT])
        x_t = sb("x_t", [P, NT])
        xn_T = sb("xn_T", [P, KC, N])
        xn_hi = sb("xn_hi", [P, KC, N], F32R)
        xn_lo = sb("xn_lo", [P, KC, N], F32R)
        v_pad = sb("v_pad", [P, NT, NP, PAIR])
        maxima = sb("maxima", [P, 2, NT, H // 2])
        shift_T = [sb(f"shift_T{k}", [H, P], F32R) for k in range(2)]
        o_n = [sb(f"o_n{k}", [P, N]) for k in range(2)]
        ident_zero = o_n[0][:, 0:P]
        x1 = sb("x1", [P, NT, D])
        mask_bc = sb("mask_bc", [P, S1])
        pad_bias = sb("pad_bias", [P, S1])
        q1 = sb("q1", [96, S1], F32R)[:]
        k1 = sb("k1", [96, S1], F32R)[:]
        head1_T = sb("head1_T", [2 * DK, S1])[:]
        kv1 = sb("kv1", [112, S1])
        sums1 = kv1[0:4 * DK]
        v1 = sb("v1", [P, QT, P], F32R)
        e1 = [sb(f"e1_{k}", [P, S1]) for k in range(2)]
        min1 = sb("min1", [P, QT])
        e1_hi = sb("e1_hi", [P, QT, P], F32R)
        e1_lo = sb("e1_lo", [P, QT, P], F32R)

        def bank(name):
            return ctx.enter_context(nc.psum_tensor(name, [P, 512], F32))
        ps_logit = [bank(f"ps_logit{k}") for k in range(2)]
        ps_max = bank("ps_max")
        ps_o = [bank(f"ps_o{k}") for k in range(2)]
        ps_a, ps_b, ps_c = bank("ps_a"), bank("ps_b"), bank("ps_c")

        s_cond, s_rows, s_wemb, s_wout, s_wo1, s_w1, s_gains = map(
            sem, ["s_cond", "s_rows", "s_wemb", "s_wout", "s_wo1", "s_w1", "s_gains"])
        s_wqkv = [sem(f"s_wqkv{k}") for k in range(KC)]
        s_x, s_resid, s_mask, s_out = map(sem, ["s_x", "s_resid", "s_mask", "s_out"])
        s_shift = [sem(f"s_shift{k}") for k in range(2)]
        s_const, s_ident, s_condT, s_condT_sb, s_mod_ps, s_mod_b, s_mod, s_wsplit, s_w1sb, s_wo1sb, s_gain = map(
            sem, ["s_const", "s_ident", "s_condT", "s_condT_sb", "s_mod_ps", "s_mod_b", "s_mod", "s_wsplit",
                  "s_w1sb", "s_wo1sb", "s_gain"])
        s_whi, s_ones, s_wdiag = sem("s_whi"), sem("s_ones"), sem("s_wdiag")
        p_xT, p_qkv, p_stack, p_max, p_maxT, p_logit, p_o, p_wout = map(
            sem, ["p_xT", "p_qkv", "p_stack", "p_max", "p_maxT", "p_logit", "p_o", "p_wout"])
        p_proj1, p_vT, p_score1, p_eT, p_o1, p_out1 = map(
            sem, ["p_proj1", "p_vT", "p_score1", "p_eT", "p_o1", "p_out1"])
        a_xms, a_xln, a_xy, a_xnT, a_raw, a_sq, a_ln, a_y, a_v, a_vpad, a_hi, a_stack, a_e, a_ohi = map(
            sem, ["a_xms", "a_xln", "a_xy", "a_xnT", "a_raw", "a_sq", "a_ln", "a_y", "a_v", "a_vpad", "a_hi",
                  "a_stack", "a_e", "a_ohi"])
        a_oln, a_oy = map(sem, ["a_oln", "a_oy"])
        a_q1, a_vT, a_v1, a_e1, a_e1hi, a_sums = map(sem, ["a_q1", "a_vT", "a_v1", "a_e1", "a_e1hi", "a_sums"])
        v_xn, v_x, v_ms, v_nt, v_y, v_qkn, v_stack, v_max, v_shift, v_oy, v_o, v_x1 = map(
            sem, ["v_xn", "v_x", "v_ms", "v_nt", "v_y", "v_qkn", "v_stack", "v_max", "v_shift", "v_oy", "v_o",
                  "v_x1"])
        v_q1, v_k1, v_v1, v_score1, v_e1lo, v_head1, v_x2 = map(
            sem, ["v_q1", "v_k1", "v_v1", "v_score1", "v_e1lo", "v_head1", "v_x2"])
        g_mod, g_xhi, g_xlo, g_kgain, g_split, g_olo = map(
            sem, ["g_mod", "g_xhi", "g_xlo", "g_kgain", "g_split", "g_olo"])
        g_pad0, g_pad, g_k1hi, g_k1lo = map(sem, ["g_pad0", "g_pad", "g_k1hi", "g_k1lo"])
        passed_pool, passed_sp, passed_dve, passed_pe = map(
            sem, ["passed_pool", "passed_sp", "passed_dve", "passed_pe"])

        block = ctx.enter_context(nc.Block())

        def steps(eng, step):
            step(None, None, None, None, 0)
            step(None, None, None, 0, 1)
            step(None, None, 0, 1, 2)
            step(None, 0, 1, 2, 3)
            with eng.Fori(2, B - 2) as i:
                step(i - 2, i - 1, i, i + 1, i + 2)
            step(B - 4, B - 3, B - 2, B - 1, None)
            step(B - 3, B - 2, B - 1, None, None)
            step(B - 2, B - 1, None, None, None)
            step(B - 1, None, None, None, None)

        @block.sync
        def _(sp):
            sp.dma_start(cond_in[:], cond).then_inc(s_cond, 16)
            sp.dma_start(rows_in[0:8, :], b_emb.rearrange("(c p) -> c p", p=P)).then_inc(s_rows, 16)
            sp.dma_start(rows_in[8:12, :], g_norm.rearrange("(c p) -> c p", p=P)).then_inc(s_rows, 16)
            w_emb_v = W_emb.rearrange("(c p) n -> p c n", p=P)

            def load_x(n):
                if not isinstance(n, int) or n > 0:
                    sp.wait_ge(p_xT, at(n, 2, 0))
                settle(sp, passed_sp, n)
                sp.dma_start(x_in[:], x[n].rearrange("(t p) d -> p t d", p=P)).then_inc(s_x, 16)

            def load_weights():
                for c in range(KC):
                    sp.dma_start(w_emb_in[:, c], w_emb_v[:, c]).then_inc(s_wemb, 16)
                w_qkv_v = W_qkv.rearrange("(c p) n -> p c n", p=P)
                for c in range(KC):
                    sp.dma_start(w_qkv_in[:, c], w_qkv_v[:, c]).then_inc(s_wqkv[c], 16)
                sp.dma_start(gq_bc[:], g_q.partition_broadcast(P)).then_inc(s_gains, 16)
                sp.dma_start(gk_bc[:], g_k.partition_broadcast(P)).then_inc(s_gains, 16)
                sp.dma_start(w_out_in[:], W_out.rearrange("(c p) n -> p c n", p=P)).then_inc(s_wout, 16)
                for k in range(2):
                    sp.dma_start(wo1_in[k * DK:(k + 1) * DK],
                                 L1_Wo.rearrange("(j i) n -> i j n", i=DK)).then_inc(s_wo1, 16)
                for k, w in enumerate((L1_Wq, L1_Wk, L1_Wv)):
                    sp.dma_start(w1_in[:, k], w[1].rearrange("(e p) d -> p e d", p=P)).then_inc(s_w1, 16)

            def shift_rows(half, batch):
                wait(sp, v_shift, at(batch, 2, half + 1))
                settle(sp, passed_sp, batch)
                h0 = half * (H // 2)
                wait(sp, p_logit, at(batch, H, -(H // 2)) if half == 0 else at(batch, H, 0))
                settle(sp, passed_sp, batch)
                for t in range(NT):
                    sp.dma_start(
                        f32(q_stack[SHIFT_ROW:SHIFT_ROW + 1, h0:h0 + H // 2, t * P:(t + 1) * P]),
                        f32(shift_T[half][t * (H // 2):(t + 1) * (H // 2), :]),
                    ).then_inc(s_shift[half], 16)

            def step(r, l, b, f, n):
                if n is not None:
                    load_x(n)
                    if isinstance(n, int) and n == 0:
                        load_weights()
                if l is not None:
                    wait(sp, v_head1, at(l, 3, 0))
                    settle(sp, passed_sp, l)
                    wait(sp, v_k1, at(l, 1, 0))
                    settle(sp, passed_sp, l)
                    wait(sp, g_pad, at(l, 1, 0))
                    settle(sp, passed_sp, l)
                    sp.dma_start(mask_bc[:], cond[l].partition_broadcast(P)).then_inc(s_mask, 16)
                if r is not None:
                    sp.wait_ge(v_x2, at(r, 2, 2))
                    settle(sp, passed_sp, r)
                    sp.dma_start(out[r].rearrange("(t p) d -> p t d", p=P), x1[:]).then_inc(s_out, 16)
                if l is not None:
                    wait(sp, s_out, at(l, 16, 0))
                    settle(sp, passed_sp, l)
                    sp.dma_start(x1[:], x[l].rearrange("(t p) d -> p t d", p=P)).then_inc(s_resid, 16)
                if b is not None:
                    shift_rows(1, b)
                if f is not None:
                    shift_rows(0, f)

            steps(sp, step)
            sp.wait_ge(s_out, 16 * B)

        @block.gpsimd
        def _(pool):
            g = nc.gpsimd
            g.memset(ident_zero, 0.0).then_inc(s_const, 1)
            g.memset(wq1[:], 0.0).then_inc(s_const, 1)
            g.memset(wk1[:], 0.0).then_inc(s_const, 1)
            g.memset(eps_col[:], EPS).then_inc(s_const, 1)
            g.memset(v_pad[:], 0.0).then_inc(s_const, 1)
            pool.wait_ge(s_const, 5)
            g.affine_select(out=ident_r[:], in_=ident_zero, compare_op=ALU.not_equal, fill=1.0, base=0,
                            pattern=[[-1, P]], channel_multiplier=1).then_inc(s_ident, 1)
            for k in (2, 6):
                g.memset(v_pad[:, :, :, k * HD:(k + 1) * HD], 1.0).then_inc(s_const, 1)

            def copy(dst, src):
                return g.tensor_scalar(dst, src, 1.0, 0.0, ALU.mult, ALU.add)

            def gains():
                pool.wait_ge(s_gains, 32)
                g.tensor_tensor(gain_bc[:], gq_bc[:], gk_bc[:], ALU.mult).then_inc(s_gain, 1)
                pool.wait_ge(s_gain, 1)
                g.tensor_scalar(gain_bc[:], gain_bc[:], HD ** -0.5, 0.0, ALU.mult, ALU.add).then_inc(s_gain, 1)
                pool.wait_ge(s_gain, 2)
                pool.wait_ge(s_wout, 16)
                for c in range(KC):
                    block_c = w_out_in[:, c, c * P:(c + 1) * P]
                    g.tensor_tensor(block_c, block_c, ident, ALU.add).then_inc(s_wdiag, 1)

            def layer1_weights():
                pool.wait_ge(s_w1, 48)
                for k in range(3):
                    g.tensor_copy(wq1[:, :, 32 * k:32 * k + DK], w1_in[:, 0]).then_inc(s_w1sb, 1)
                    g.tensor_copy(wk1[:, :, 32 * k:32 * k + DK], w1_in[:, 1]).then_inc(s_w1sb, 1)
                g.tensor_copy(wq1[:, :, 96:96 + DK], w1_in[:, 2]).then_inc(s_w1sb, 1)

            def modulation(n):
                wait(pool, a_xnT, at(n, 4, 0))
                settle(pool, passed_pool, n)
                pool.wait_ge(s_mod, 2)
                g.tensor_copy(mod_cur[:], mod_all[:, n]).then_inc(g_mod, 1)

            def x_split(n):
                pool.wait_ge(a_xnT, at(n, 4, 4))
                settle(pool, passed_pool, n)
                if not isinstance(n, int) or n > 0:
                    pool.wait_ge(p_qkv, at(n, 6, 0))
                    settle(pool, passed_pool, n)
                copy(xn_hi[:], xn_T[:]).then_inc(g_xhi, 1)
                pool.wait_ge(g_xhi, at(n, 1, 1))
                g.tensor_tensor(xn_lo[:], xn_T[:], f32(xn_hi[:]), ALU.subtract).then_inc(g_xlo, 1)

            def k_gain(f, t):
                pool.wait_ge(a_raw, at(f, 4, 2 * t + 2))
                k = qk_raw[:, t, 1].rearrange("p (h d) -> p h d", d=HD)
                gain = gain_bc[:].unsqueeze(1).to_broadcast([P, H, HD])
                g.tensor_tensor(k, k, gain, ALU.mult).then_inc(g_kgain, 1)

            def split(f, j):
                t, k = j // 2, j % 2
                dst = qk_split[:, k, t]
                val = qk_raw[:, t, k].rearrange("p (h d) -> p h d", d=HD)
                lo, again = (1, 2) if k == 0 else (2, 1)
                pool.wait_ge(a_hi, at(f, 4, j + 1))
                g.tensor_tensor(dst[:, :, lo * HD:(lo + 1) * HD], val, f32(dst[:, :, 0:HD]),
                                ALU.subtract).then_inc(g_split, 1)
                copy(dst[:, :, again * HD:(again + 1) * HD], f32(dst[:, :, 0:HD])).then_inc(g_split, 1)

            def o_lo_part(b, grp):
                pool.wait_ge(a_ohi, at(b, NG, grp + 1))
                g.tensor_tensor(o_lo[:, grp], o_n[grp % 2][:], f32(o_hi[:, grp]), ALU.subtract).then_inc(g_olo, 1)

            def mask_bias(l):
                pool.wait_ge(s_mask, at(l, 16, 16))
                settle(pool, passed_pool, l)
                wait(pool, v_score1, at(l, 4, 0))
                settle(pool, passed_pool, l)
                g.tensor_scalar(pad_bias[:], mask_bc[:], -1.0, 1.0, ALU.mult, ALU.add).then_inc(g_pad0, 1)
                pool.wait_ge(g_pad0, at(l, 1, 1))
                settle(pool, passed_pool, l)
                g.tensor_scalar(pad_bias[:], pad_bias[:], NEG, 0.0, ALU.mult, ALU.add).then_inc(g_pad, 1)

            def k1_split(l):
                pool.wait_ge(v_k1, at(l, 1, 1))
                settle(pool, passed_pool, l)
                copy(k1, kv1[0:96]).then_inc(g_k1hi, 1)
                pool.wait_ge(g_k1hi, at(l, 1, 1))
                g.tensor_tensor(k1[64:96], kv1[64:96], f32(k1[64:96]), ALU.subtract).then_inc(g_k1lo, 1)
                pool.wait_ge(g_k1lo, at(l, 1, 1))

            def step(r, l, b, f, n):
                if f is not None and isinstance(f, int) and f == 0:
                    gains()
                    layer1_weights()
                if n is not None and isinstance(n, int) and n == 0:
                    modulation(n)
                for s in range(H):
                    if l is not None and s == 1:
                        o_lo_part(l, NG - 1)
                    if f is not None and s in (1, 3):
                        k_gain(f, s // 2)
                    if f is not None and s in HI_SLOTS:
                        split(f, HI_SLOTS[s])
                    if l is not None and s == 4:
                        mask_bias(l)
                    if l is not None and s == 7:
                        k1_split(l)
                    if b is not None and s in (6, 9, 13):
                        o_lo_part(b, s // 4 - 1)
                    if n is not None and s == 9 and not (isinstance(n, int) and n == 0):
                        modulation(n)
                    if n is not None and s == 13:
                        x_split(n)

            steps(pool, step)

        @block.scalar
        def _(act):
            a = nc.scalar
            a.preload_act_table_set("natural_log_exp_and_others")
            act.wait_ge(s_const, 7)

            def weights_hi():
                for c in range(KC):
                    act.wait_ge(s_wqkv[c], 16)
                    a.activation(wqkv_hi[:, c], w_qkv_in[:, c], ACT.Copy).then_inc(s_whi, 1)

            def wout_hi_part():
                act.wait_ge(s_wdiag, KC)
                a.activation(wout_hi[:], w_out_in[:], ACT.Copy).then_inc(s_whi, 1)

            def x_squares(n, t):
                act.wait_ge(s_x, at(n, 16, 16))
                wait(act, v_x, at(n, 2, 0))
                wait(act, g_xlo, at(n, 1, 0))
                a.activation(xn_T[:, 2 * t:2 * t + 2].rearrange("p c n -> p (c n)"), x_in[:, t], ACT.Square,
                             scale=D ** -0.5, accum_out=x_ms[:, t:t + 1]).then_inc(a_xms, 1)

            def x_rsqrt(n):
                act.wait_ge(a_xms, at(n, 2, 2))
                wait(act, v_x, at(n, 2, 0))
                a.activation(x_y[:], x_ms[:], ACT.Ln, bias=eps_col[:]).then_inc(a_xln, 1)
                act.wait_ge(a_xln, at(n, 1, 1))
                a.activation(x_y[:], x_y[:], ACT.Exp, scale=-0.5).then_inc(a_xy, 1)

            def modulate(n, j):
                act.wait_ge(g_mod, at(n, 1, 1))
                act.wait_ge(p_xT, at(n, 2, j + 1))
                for c in (2 * j, 2 * j + 1):
                    a.activation(xn_T[:, c], (ps_a, ps_b)[j][:, (c % 2) * N:(c % 2 + 1) * N], ACT.Identity,
                                 scale=mod_cur[:, c:c + 1], bias=mod_cur[:, KC + c:KC + c + 1]).then_inc(a_xnT, 1)

            def qk_out(f, j):
                t, k = j // 2, j % 2
                act.wait_ge(p_qkv, at(f, 6, j + 1))
                wait(act, g_split, at(f, 8, 0))
                a.activation(qk_raw[:, t, k], ps_a[:], ACT.Copy).then_inc(a_raw, 1)
                wait(act, v_ms, at(f, 4, j))
                wait(act, a_vpad, at(f, 2, 0))
                a.activation(squares, ps_a[:], ACT.Square, scale=HD ** -0.5).then_inc(a_sq, 1)

            def qk_rsqrt(f, j):
                act.wait_ge(v_ms, at(f, 4, j + 1))
                wait(act, v_qkn, at(f, 4, 0))
                a.activation(head_y[:, j], head_ms[:, j], ACT.Ln, bias=eps_col[:]).then_inc(a_ln, 1)
                act.wait_ge(a_ln, at(f, 4, j + 1))
                a.activation(head_y[:, j], head_y[:, j], ACT.Exp, scale=-0.5).then_inc(a_y, 1)

            def qk_hi(f, j):
                t, k = j // 2, j % 2
                act.wait_ge(v_qkn, at(f, 4, j + 1))
                wait(act, p_stack, at(f, 4 * NG, 0))
                a.activation(qk_split[:, k, t, :, 0:HD], qk_raw[:, t, k].rearrange("p (h d) -> p h d", d=HD),
                             ACT.Copy).then_inc(a_hi, 1)

            def v_out(f, t):
                act.wait_ge(p_qkv, at(f, 6, 5 + t))
                act.wait_ge(v_ms, at(f, 4, 4))
                a.activation(v_raw[:, t], ps_a[:], ACT.Copy).then_inc(a_v, 1)

            def v_place(b, t):
                act.wait_ge(a_v, at(b, 2, 2))
                wait(act, p_o, at(b, H, 0))
                src = v_raw[:, t].rearrange("p (m k d) -> p m k d", k=2, d=HD)
                for k in range(2):
                    ins = a.activation(v_pad[:, t, :, 4 * k * HD:(4 * k + 1) * HD], src[:, :, k], ACT.Copy)
                ins.then_inc(a_vpad, 1)

            def stack_out(f, j, ps):
                grp, k, t = j // 4, j // 2 % 2, j % 2
                dst = (q_stack, k_stack)[k]
                act.wait_ge(p_stack, at(f, 4 * NG, j + 1))
                a.activation(dst[0:SHIFT_ROW, grp * G:(grp + 1) * G, t * P:(t + 1) * P],
                             ps[0:SHIFT_ROW, :].rearrange("p (h n) -> p h n", h=G), ACT.Copy).then_inc(a_stack, 1)

            def exp(b, h):
                act.wait_ge(p_logit, at(b, H, h + 1))
                wait(act, p_o, at(b, H, h - 1) if h >= 2 else at(b, H, 0))
                a.activation(e[h % 2][:].rearrange("p t n -> p (t n)"), ps_logit[h % 2][:],
                             ACT.Exp).then_inc(a_e, 1)

            def o_reciprocal(b, pair):
                grp, k = pair // 2, pair % 2
                act.wait_ge(p_o, at(b, H, 2 * pair + 2))
                wait(act, g_olo, at(b, NG, grp - 1) if grp >= 2 else at(b, NG, 0))
                o = o_n[grp % 2][k * 2 * HD:(k + 1) * 2 * HD, :]
                a.activation(o, ps_o[pair % 2][2 * HD:4 * HD, 0:N], ACT.Ln).then_inc(a_oln, 1)
                act.wait_ge(a_oln, at(b, NP, pair + 1))
                a.activation(o, o, ACT.Exp, scale=-1.0).then_inc(a_oy, 1)

            def o_hi_part(b, grp):
                act.wait_ge(v_o, at(b, NP, 2 * grp + 2))
                wait(act, p_wout, at(b, 2, 0))
                a.activation(o_hi[:, grp], o_n[grp % 2][:], ACT.Copy).then_inc(a_ohi, 1)

            def q1_out(l):
                act.wait_ge(p_proj1, at(l, 2, 1))
                wait(act, p_score1, at(l, 4, 0))
                a.activation(q1, ps_c[0:96, :], ACT.Copy, scale=-(DK ** -0.5)).then_inc(a_q1, 1)
                wait(act, p_vT, at(l, 1, 0))
                a.activation(kv1[96:112], ps_c[96:112, :], ACT.Copy).then_inc(a_vT, 1)

            def v1_hi(l):
                act.wait_ge(p_vT, at(l, 1, 1))
                wait(act, p_o1, at(l, 4, 0))
                a.activation(v1[:, :, 0:DK], ps_c[:, 0:QT * DK].rearrange("p (t d) -> p t d", d=DK),
                             ACT.Copy).then_inc(a_v1, 1)

            def exp1(l, q):
                act.wait_ge(v_score1, at(l, 4, q + 1))
                a.activation(e1[q % 2][:], e1[q % 2][:], ACT.Exp, scale=-1.0,
                             bias=min1[:, q:q + 1]).then_inc(a_e1, 1)

            def e1_hi_out(l, q):
                act.wait_ge(p_eT, at(l, 4, q + 1))
                wait(act, p_o1, at(l, 4, q))
                a.activation(e1_hi[:].rearrange("p t n -> p (t n)"), ps_b[:], ACT.Copy).then_inc(a_e1hi, 1)

            def sums1_out(l, q):
                act.wait_ge(p_o1, at(l, 4, q + 1))
                if q == 0:
                    act.wait_ge(g_k1lo, at(l, 1, 1))
                a.activation(sums1[:, q * P:(q + 1) * P], ps_c[0:4 * DK, 0:P], ACT.Copy).then_inc(a_sums, 1)

            def step(r, l, b, f, n):
                if n is not None and isinstance(n, int) and n == 0:
                    x_squares(n, 0)
                    x_squares(n, 1)
                    x_rsqrt(n)
                    weights_hi()
                if f is not None and isinstance(f, int) and f == 0:
                    wout_hi_part()
                for s in range(H):
                    if b is not None:
                        exp(b, s)
                    if s == 0 and l is not None:
                        o_reciprocal(l, NP - 1)
                    if s == 0 and b is not None:
                        v_place(b, 0)
                        v_place(b, 1)
                    if b is not None and s in STACK3_SLOTS:
                        stack_out(b, STACK3_SLOTS[s][0], ps_b)
                    if f is not None and s in NORM_SLOTS:
                        qk_rsqrt(f, NORM_SLOTS[s])
                    if l is not None and s == 1:
                        o_hi_part(l, NG - 1)
                    if f is not None and QKV_SLOTS.get(s, 9) < 4:
                        qk_out(f, QKV_SLOTS[s])
                    if f is not None and s in HI_SLOTS:
                        qk_hi(f, HI_SLOTS[s])
                    if f is not None and 4 <= QKV_SLOTS.get(s, 9) < 6:
                        v_out(f, QKV_SLOTS[s] - 4)
                    if f is not None and s in STACK_SLOTS:
                        stack_out(f, STACK_SLOTS[s][0], ps_a)
                    if b is not None and s in (6, 9, 13):
                        o_hi_part(b, s // 4 - 1)
                    if l is not None:
                        if s == 6:
                            q1_out(l)
                        if s == 8:
                            v1_hi(l)
                        if s in PV1_SLOTS:
                            sums1_out(l, PV1_SLOTS[s])
                        if s in E1T_SLOTS:
                            e1_hi_out(l, E1T_SLOTS[s])
                        if s - 1 in SCORE1_SLOTS:
                            exp1(l, SCORE1_SLOTS[s - 1])
                    if n is not None and not (isinstance(n, int) and n == 0):
                        if s in (7, 8):
                            x_squares(n, s - 7)
                        if s == 9:
                            x_rsqrt(n)
                    if n is not None and s in XT_SLOTS:
                        modulate(n, XT_SLOTS[s])
                    if b is not None and s % 2 == 0 and s >= 2:
                        o_reciprocal(b, s // 2 - 1)

            steps(act, step)

        @block.vector
        def _(dve):
            v = nc.vector
            dve.wait_ge(s_condT, 1)
            v.tensor_copy(cond_T[:].rearrange("p b c -> p c b"),
                          ps_a[:, 0:KC * B].rearrange("p (c b) -> p c b", b=B)).then_inc(s_condT_sb, 1)
            v.tensor_copy(biasgain_T[:], ps_a[:, 64:76]).then_inc(s_condT_sb, 1)

            def all_modulations():
                dve.wait_ge(s_condT_sb, 2)
                dve.wait_ge(s_mod_ps, 1)
                v.tensor_tensor(mod_all[:].rearrange("p b c -> p c b"),
                                ps_b[:, 0:2 * KC * B].rearrange("p (c b) -> p c b", b=B),
                                biasgain_T[:, 0:8].unsqueeze(2).to_broadcast([P, 8, B]), ALU.add).then_inc(s_mod_b, 1)
                dve.wait_ge(s_mod_b, 1)
                v.tensor_scalar(mod_all[:, :, 0:KC], mod_all[:, :, 0:KC], 1.0, None, ALU.add).then_inc(s_mod, 1)
                dve.wait_ge(s_mod, 1)
                v.tensor_tensor(mod_all[:, :, 0:KC], mod_all[:, :, 0:KC],
                                biasgain_T[:, 8:12].unsqueeze(1).to_broadcast([P, B, KC]), ALU.mult).then_inc(s_mod, 1)

            def weights_lo():
                for c in range(KC):
                    dve.wait_ge(s_whi, c + 1)
                    v.tensor_tensor(wqkv_lo[:, c], w_qkv_in[:, c], f32(wqkv_hi[:, c]),
                                    ALU.subtract).then_inc(s_wsplit, 1)

            def more_weights():
                dve.wait_ge(s_whi, KC + 1)
                v.tensor_tensor(wout_lo[:], w_out_in[:], f32(wout_hi[:]), ALU.subtract).then_inc(s_wsplit, 1)
                dve.wait_ge(s_wo1, 32)
                v.tensor_reduce(wo1, wo1_in[:].rearrange("i j n -> i n j"), AX.X, ALU.add).then_inc(s_wo1sb, 1)
                dve.wait_ge(s_wsplit, KC + 1)
                dve.wait_ge(s_wo1sb, 1)
                v.memset(f32(k_stack[SHIFT_ROW:SHIFT_ROW + 1, :, :]), 1.0).then_inc(s_ones, 1)
                v.memset(f32(v1[:, :, 2 * DK:]), 1.0).then_inc(s_ones, 1)

            def newton(y, ms, t, count, seen):
                v.tensor_tensor(t, y, y, ALU.mult).then_inc(count, 1)
                dve.wait_ge(count, seen(1))
                v.scalar_tensor_tensor(out=t, in0=ms, scalar=EPS, in1=t, op0=ALU.add, op1=ALU.mult).then_inc(count, 1)
                dve.wait_ge(count, seen(2))
                v.tensor_scalar(t, t, -0.5, 1.5, ALU.mult, ALU.add).then_inc(count, 1)
                dve.wait_ge(count, seen(3))
                return v.tensor_tensor(y, y, t, ALU.mult)

            def x_normalise(n):
                dve.wait_ge(a_xy, at(n, 1, 1))
                newton(x_y[:], x_ms[:], x_t[:], v_xn, lambda k: at(n, 4, k)).then_inc(v_xn, 1)
                dve.wait_ge(v_xn, at(n, 4, 4))
                for t in range(NT):
                    v.tensor_scalar(x_in[:, t], x_in[:, t], x_y[:, t:t + 1], None, ALU.mult).then_inc(v_x, 1)

            def mean_squares(f, j):
                dve.wait_ge(a_sq, at(f, 4, j + 1))
                v.tensor_reduce(head_ms[:, j], squares.rearrange("p (h d) -> p h d", d=HD),
                                AX.X, ALU.add).then_inc(v_ms, 1)

            def qk_norm(f, j):
                t, k = j // 2, j % 2
                dve.wait_ge(a_y, at(f, 4, j + 1))
                newton(head_y[:, j], head_ms[:, j], head_t[:], v_nt, lambda m: at(f, 12, 3 * j + m)).then_inc(v_y, 1)
                dve.wait_ge(v_y, at(f, 4, j + 1))
                dve.wait_ge(a_raw, at(f, 4, j + 1))
                if k == 1:
                    dve.wait_ge(g_kgain, at(f, 2, t + 1))
                val = qk_raw[:, t, k].rearrange("p (h d) -> p h d", d=HD)
                v.tensor_tensor(val, val, head_y[:, j].unsqueeze(2).to_broadcast([P, H, HD]),
                                ALU.mult).then_inc(v_qkn, 1)

            def stack_out(f, j, ps):
                grp, k, t = j // 4, j // 2 % 2, j % 2
                dst = (q_stack, k_stack)[k]
                dve.wait_ge(p_stack, at(f, 4 * NG, j + 1))
                v.tensor_copy(dst[0:SHIFT_ROW, grp * G:(grp + 1) * G, t * P:(t + 1) * P],
                              ps[0:SHIFT_ROW, :].rearrange("p (h n) -> p h n", h=G)).then_inc(v_stack, 1)

            def row_max(b, h):
                dve.wait_ge(p_max, at(b, H, h + 1))
                v.tensor_reduce(maxima[:, h // 8, :, h % 8], ps_max[:].rearrange("p (t n) -> p t n", t=NT),
                                AX.X, ALU.max).then_inc(v_max, 1)

            def shift_out(batch, half):
                dve.wait_ge(p_maxT, at(batch, 2, half + 1))
                wait(dve, s_shift[half], at(batch, 32, 0))
                v.tensor_scalar(shift_T[half][:], (ps_b, ps_c)[half][0:H, 0:P], -1.0, None, ALU.mult).then_inc(v_shift, 1)

            def o_norm(b, pair):
                grp, k = pair // 2, pair % 2
                dve.wait_ge(a_oy, at(b, NP, pair + 1))
                ps = ps_o[pair % 2]
                o = o_n[grp % 2][k * 2 * HD:(k + 1) * 2 * HD, :]
                sums, dens = ps[0:2 * HD, 0:N], ps[2 * HD:4 * HD, 0:N]
                v.scalar_tensor_tensor(out=dens, in0=dens, scalar=-1.0, in1=o, op0=ALU.mult,
                                       op1=ALU.mult).then_inc(v_oy, 1)
                v.tensor_tensor(o, sums, o, ALU.mult).then_inc(v_oy, 1)
                dve.wait_ge(v_oy, at(b, 2 * NP, 2 * pair + 2))
                v.scalar_tensor_tensor(out=o, in0=dens, scalar=2.0, in1=o, op0=ALU.add,
                                       op1=ALU.mult).then_inc(v_o, 1)

            def x1_out(l, t):
                dve.wait_ge(p_wout, at(l, 2, t + 1))
                dve.wait_ge(s_resid, at(l, 16, 16))
                v.tensor_tensor(x1[:, t], (ps_b, ps_c)[t][:], x1[:, t], ALU.add).then_inc(v_x1, 1)

            def q1_lo(l):
                dve.wait_ge(a_q1, at(l, 1, 1))
                dve.wait_ge(a_vT, at(l, 1, 1))
                v.scalar_tensor_tensor(out=q1[32:64], in0=ps_c[32:64, :], scalar=-(DK ** -0.5),
                                       in1=f32(q1[32:64]), op0=ALU.mult, op1=ALU.subtract).then_inc(v_q1, 1)

            def k1_mask(l):
                dve.wait_ge(p_proj1, at(l, 2, 2))
                dve.wait_ge(s_mask, at(l, 16, 16))
                wait(dve, v_head1, at(l, 3, 0))
                v.tensor_tensor(kv1[0:96], ps_c[0:96, :], mask_bc[0:96, :], ALU.mult).then_inc(v_k1, 1)

            def v1_lo(l):
                dve.wait_ge(a_v1, at(l, 1, 1))
                v.tensor_tensor(v1[:, :, DK:2 * DK], ps_c[:, 0:QT * DK].rearrange("p (t d) -> p t d", d=DK),
                                f32(v1[:, :, 0:DK]), ALU.subtract).then_inc(v_v1, 1)

            def score1(l, q):
                dve.wait_ge(p_score1, at(l, 4, q + 1))
                dve.wait_ge(g_pad, at(l, 1, 1))
                wait(dve, p_eT, at(l, 4, q - 1) if q >= 2 else at(l, 4, 0))
                settle(dve, passed_dve, l)
                v.tensor_tensor_reduce(out=e1[q % 2][:], in0=ps_c[:], in1=pad_bias[:], scale=1.0, scalar=3e38,
                                       op0=ALU.add, op1=ALU.min, accum_out=min1[:, q:q + 1]).then_inc(v_score1, 1)

            def e1_lo_out(l, q):
                dve.wait_ge(a_e1hi, at(l, 4, q + 1))
                v.tensor_tensor(e1_lo[:].rearrange("p t n -> p (t n)"), ps_b[:],
                                f32(e1_hi[:]).rearrange("p t n -> p (t n)"), ALU.subtract).then_inc(v_e1lo, 1)

            def head1_out(r):
                dve.wait_ge(a_sums, at(r, 4, 4))
                wait(dve, p_out1, at(r, 2, 0))
                v.reciprocal(head1_T, sums1[2 * DK:4 * DK]).then_inc(v_head1, 1)
                dve.wait_ge(v_head1, at(r, 3, 1))
                v.tensor_tensor(head1_T, head1_T, sums1[0:2 * DK], ALU.mult).then_inc(v_head1, 1)
                dve.wait_ge(v_head1, at(r, 3, 2))
                v.tensor_tensor(head1_T, head1_T, mask_bc[0:2 * DK], ALU.mult).then_inc(v_head1, 1)

            def x2_out(r, t):
                dve.wait_ge(p_out1, at(r, 2, t + 1))
                v.tensor_tensor(x1[:, t], (ps_b, ps_c)[t][:], x1[:, t], ALU.add).then_inc(v_x2, 1)

            def step(r, l, b, f, n):
                if n is not None and isinstance(n, int) and n == 0:
                    x_normalise(n)
                    all_modulations()
                    weights_lo()
                if f is not None and isinstance(f, int) and f == 0:
                    more_weights()
                for s in range(H):
                    if b is not None and s in MAX3_SLOTS:
                        row_max(b, MAX3_SLOTS[s][0])
                    if f is not None and s in MAX_SLOTS:
                        row_max(f, MAX_SLOTS[s][0])
                    if f is not None and s in NORM_SLOTS:
                        qk_norm(f, NORM_SLOTS[s])
                    if f is not None and QKV_SLOTS.get(s, 9) < 4:
                        mean_squares(f, QKV_SLOTS[s])
                    if r is not None and s == 0:
                        head1_out(r)
                    if l is not None and s in WOUT_SLOTS:
                        x1_out(l, WOUT_SLOTS[s])
                    if r is not None and s == 2:
                        x2_out(r, 0)
                        x2_out(r, 1)
                    if l is not None:
                        if s == 6:
                            q1_lo(l)
                        if s == 7:
                            k1_mask(l)
                        if s == 8:
                            v1_lo(l)
                        if s in E1T_SLOTS:
                            e1_lo_out(l, E1T_SLOTS[s])
                        if s in SCORE1_SLOTS:
                            score1(l, SCORE1_SLOTS[s])
                    if b is not None and s in MAX3_SLOTS:
                        row_max(b, MAX3_SLOTS[s][1])
                    if f is not None and s in MAX_SLOTS:
                        row_max(f, MAX_SLOTS[s][1])
                    if b is not None and s in STACK3_SLOTS:
                        stack_out(b, STACK3_SLOTS[s][1], ps_c)
                    if f is not None and s in STACK_SLOTS:
                        stack_out(f, STACK_SLOTS[s][1], ps_b)
                    if s == 4 and b is not None:
                        shift_out(b, 1)
                    if l is not None and s == 0:
                        o_norm(l, NP - 1)
                    if b is not None and s % 2 == 0 and s >= 2:
                        o_norm(b, s // 2 - 1)
                    if n is not None and s == 10 and not (isinstance(n, int) and n == 0):
                        x_normalise(n)
                    if s == 14 and f is not None:
                        shift_out(f, 0)

            steps(dve, step)

        @block.tensor
        def _(pe):
            mm, tr = nc.tensor.matmul, nc.tensor.transpose
            pe.wait_ge(s_ident, 1)
            pe.wait_ge(s_cond, 16)
            pe.wait_ge(s_rows, 32)
            for c in range(KC):
                tr(ps_a[:, c * B:(c + 1) * B], cond_in[:, c * P:(c + 1) * P], ident[0:B, 0:B])
            tr(ps_a[:, 64:76], rows_in[0:12, :], ident[0:12, 0:12]).then_inc(s_condT, 1)

            def modulation_product():
                pe.wait_ge(s_condT_sb, 2)
                pe.wait_ge(s_wemb, 16 * KC)
                for m in range(2 * KC):
                    for c in range(KC):
                        ins = mm(ps_b[:, m * B:(m + 1) * B], w_emb_in[:, c, m * P:(m + 1) * P], cond_T[:, :, c],
                                 start=(c == 0), stop=(c == KC - 1))
                ins.then_inc(s_mod_ps, 1)

            def product3(ps, a_hi_, a_lo_, w_hi_, w_lo_, toks, cols, part):
                todo = [(a, w, c) for c in range(KC) for a, w in ((a_hi_, w_hi_), (a_lo_, w_hi_), (a_hi_, w_lo_))]
                half = len(todo) // 2
                for n in range(part * half, (part + 1) * half):
                    a, w, c = todo[n]
                    ins = mm(ps[:], a[:, c, toks], w[:, c, cols], start=(n == 0), stop=(n == len(todo) - 1))
                return ins

            freed = {"a": (s_condT_sb, 2), "b": (s_mod_b, 1), "c": None}

            def use(name, reader, value):
                if freed[name] is not None:
                    wait(pe, *freed[name])
                freed[name] = (reader, value)
                return {"a": ps_a, "b": ps_b, "c": ps_c}[name]

            def x_T(n, j):
                ps = use("ab"[j], a_xnT, at(n, 4, 2 * j + 2))
                pe.wait_ge(v_x, at(n, 2, 2))
                for c in range(2):
                    for t in range(NT):
                        ins = tr(ps[:, c * N + t * P:c * N + (t + 1) * P],
                                 x_in[:, t, (2 * j + c) * P:(2 * j + c + 1) * P], ident)
                ins.then_inc(p_xT, 1)

            def qkv_product(f, j, part):
                t = j // 2 if j < 4 else j - 4
                k = j % 2 if j < 4 else 2
                if part == 0:
                    use("a", *((a_sq, at(f, 4, j + 1)) if j < 4 else (a_v, at(f, 2, j - 3))))
                    pe.wait_ge(g_xlo, at(f, 1, 1))
                ins = product3(ps_a, xn_hi, xn_lo, wqkv_hi, wqkv_lo, slice(t * P, (t + 1) * P),
                               slice(k * D, (k + 1) * D), part)
                if part == 1:
                    ins.then_inc(p_qkv, 1)

            def out_product(l, t, part):
                if part == 0:
                    use("bc"[t], v_x1, at(l, 2, t + 1))
                    pe.wait_ge(g_olo, at(l, NG, NG))
                ins = product3((ps_b, ps_c)[t], o_hi, o_lo, wout_hi, wout_lo, slice(t * P, (t + 1) * P), slice(0, D), part)
                if part == 1:
                    ins.then_inc(p_wout, 1)

            def stack(f, j):
                grp, k, t = j // 4, j // 2 % 2, j % 2
                name = ("ab" if grp < NG - 1 else "bc")[j % 2]
                ps = use(name, (a_stack, v_stack)[j % 2], at(f, 8, j // 2 + 1))
                pe.wait_ge(g_split, at(f, 8, 2 * (2 * t + k) + 2))
                for h in range(G):
                    ins = tr(ps[0:SHIFT_ROW, h * P:(h + 1) * P].bitcast(F32R), qk_split[:, k, t, grp * G + h, :],
                             ident_r[:])
                ins.then_inc(p_stack, 1)

            def max_logits(b, h):
                wait(pe, v_max, at(b, H, h))
                pe.wait_ge(a_stack, at(b, 8, 2 * (h // G + 1)))
                pe.wait_ge(v_stack, at(b, 8, 2 * (h // G + 1)))
                for t in range(NT):
                    ins = mm(ps_max[:, t * N:(t + 1) * N], q_stack[0:SHIFT_ROW, h, t * P:(t + 1) * P],
                             k_stack[0:SHIFT_ROW, h, :], start=True, stop=True)
                ins.then_inc(p_max, 1)

            def max_T(batch, half):
                ps = use("bc"[half], v_shift, at(batch, 2, half + 1))
                pe.wait_ge(v_max, at(batch, H, (half + 1) * (H // 2)))
                tr(ps[0:H, 0:P], maxima[:, half].rearrange("p t h -> p (t h)"), ident).then_inc(p_maxT, 1)

            def logits(b, h):
                wait(pe, a_e, at(b, H, h - 1))
                pe.wait_ge(s_shift[h // 8], at(b, 32, 32))
                for t in range(NT):
                    ins = mm(ps_logit[h % 2][:, t * N:(t + 1) * N], k_stack[:, h, t * P:(t + 1) * P],
                             q_stack[:, h, :], start=True, stop=True)
                ins.then_inc(p_logit, 1)

            def weighted_v(b, h):
                pair, odd = h // 2, h % 2
                if odd == 0:
                    wait(pe, v_o, at(b, NP, pair - 1))
                pe.wait_ge(a_e, at(b, H, h + 1))
                pe.wait_ge(a_vpad, at(b, 2, 2))
                for t in range(NT):
                    lhsT = v_pad[:, t, pair, odd * ODD:odd * ODD + P]
                    ins = mm(ps_o[pair % 2][:, 0:N], lhsT, e[h % 2][:, t, :],
                             start=(odd == 0 and t == 0), stop=(odd == 1 and t == NT - 1))
                ins.then_inc(p_o, 1)

            def project1(l, k):
                w, m = ((wq1, 112), (wk1, 96))[k]
                ps = use("c", (v_q1, v_k1)[k], at(l, 1, 1))
                pe.wait_ge(v_x1, at(l, 2, 2))
                for t in range(ET):
                    ins = mm(ps[0:m, :], w[:, t, :], x1[:, t, :], start=(t == 0), stop=(t == ET - 1))
                ins.then_inc(p_proj1, 1)

            def v1_T(l):
                ps = use("c", v_v1, at(l, 1, 1))
                pe.wait_ge(a_vT, at(l, 1, 1))
                settle(pe, passed_pe, l)
                for t in range(QT):
                    ins = tr(ps[:, t * DK:(t + 1) * DK], kv1[96:112, t * P:(t + 1) * P], ident[96:112, 96:112])
                ins.then_inc(p_vT, 1)

            def scores1(l, q):
                ps = use("c", v_score1, at(l, 4, q + 1))
                pe.wait_ge(v_q1, at(l, 1, 1))
                pe.wait_ge(g_k1lo, at(l, 1, 1))
                mm(ps[:], q1[:, q * P:(q + 1) * P], k1, start=True, stop=True).then_inc(p_score1, 1)

            def e1_transposes(l, q):
                ps = use("b", v_e1lo, at(l, 4, q + 1))
                pe.wait_ge(a_e1, at(l, 4, q + 1))
                for t in range(QT):
                    ins = tr(ps[:, t * P:(t + 1) * P], e1[q % 2][:, t * P:(t + 1) * P], ident)
                ins.then_inc(p_eT, 1)

            def weighted_v1(l, q):
                ps = use("c", a_sums, at(l, 4, q + 1))
                pe.wait_ge(v_e1lo, at(l, 4, q + 1))
                pe.wait_ge(v_v1, at(l, 1, 1))
                for t in range(QT):
                    mm(ps[:, 0:P], v1[:, t, :], e1_hi[:, t, :], start=(t == 0), stop=False)
                    ins = mm(ps[:, 0:P], v1[:, t, :], e1_lo[:, t, :], start=False, stop=(t == QT - 1))
                ins.then_inc(p_o1, 1)

            def out1(r, t):
                ps = use("bc"[t], v_x2, at(r, 2, t + 1))
                pe.wait_ge(v_head1, at(r, 3, 3))
                mm(ps[:], wo1[:, t * P:(t + 1) * P], head1_T, start=True, stop=True).then_inc(p_out1, 1)

            def step(r, l, b, f, n):
                if n is not None and isinstance(n, int) and n == 0:
                    modulation_product()
                if b is not None:
                    freed["a"] = (a_stack, at(b, 8, 6))
                    freed["b"] = (v_shift, at(b, 2, 1))
                if r is not None:
                    freed["c"] = (a_sums, at(r, 4, 4))
                if f is not None and isinstance(f, int) and f == 0:
                    pe.wait_ge(s_wsplit, KC)
                if b is not None and isinstance(b, int) and b == 0:
                    pe.wait_ge(s_ones, 2)
                if l is not None and isinstance(l, int) and l == 0:
                    pe.wait_ge(s_wsplit, KC + 1)
                    pe.wait_ge(s_w1sb, 7)
                    pe.wait_ge(s_wo1sb, 1)
                for s in range(H):
                    def products(part):
                        if f is not None and s in QKV_SLOTS:
                            qkv_product(f, QKV_SLOTS[s], part)
                        if l is not None and s in WOUT_SLOTS:
                            out_product(l, WOUT_SLOTS[s], part)

                    def stacks(k):
                        if b is not None and s in STACK3_SLOTS:
                            stack(b, STACK3_SLOTS[s][k])
                        if f is not None and s in STACK_SLOTS:
                            stack(f, STACK_SLOTS[s][k])

                    def maxima_products(k):
                        if b is not None and s in MAX3_SLOTS:
                            max_logits(b, MAX3_SLOTS[s][k])
                        if f is not None and s in MAX_SLOTS:
                            max_logits(f, MAX_SLOTS[s][k])

                    products(0)
                    if b is not None:
                        logits(b, s)
                    maxima_products(0)
                    products(1)
                    stacks(0)
                    if b is not None and s >= 1:
                        weighted_v(b, s - 1)
                    if l is not None and s == 0:
                        weighted_v(l, H - 1)
                    if r is not None and s == 2:
                        out1(r, 0)
                        out1(r, 1)
                    if l is not None:
                        if s in PROJ1_SLOTS:
                            project1(l, PROJ1_SLOTS[s])
                        if s == 8:
                            v1_T(l)
                        if s in PV1_SLOTS:
                            weighted_v1(l, PV1_SLOTS[s])
                        if s in E1T_SLOTS:
                            e1_transposes(l, E1T_SLOTS[s])
                        if s in SCORE1_SLOTS:
                            scores1(l, SCORE1_SLOTS[s])
                    maxima_products(1)
                    stacks(1)
                    if s in MAX_T_SLOTS:
                        half = MAX_T_SLOTS[s]
                        batch = f if half == 0 else b
                        if batch is not None:
                            max_T(batch, half)
                    if n is not None and s in XT_SLOTS:
                        x_T(n, XT_SLOTS[s])

            steps(pe, step)


_INS = ['x', 'cond_2048', 'L0_cond_W_emb', 'L0_cond_b_emb', 'L0_cond_g_norm', 'L0_cond_W_qkv', 'L0_cond_g_q',
        'L0_cond_g_k', 'L0_cond_W_out', 'L1_cond_Wq', 'L1_cond_Wk', 'L1_cond_Wv', 'L1_cond_Wo']
_OUT = ((B, N, D), 'float32')


def kernel(**inputs):
    import numpy as _np
    import concourse.bacc as _bacc
    from concourse import mybir as _mybir
    from concourse.bass_utils import run_bass_kernel_spmd as _run

    nc = _bacc.Bacc("TRN2", target_bir_lowering=False, num_devices=1)
    arrays, args = {}, []
    for name in _INS:
        a = _np.ascontiguousarray(inputs[name])
        arrays[f"in_{name}_dram"] = a
        args.append(nc.dram_tensor(f"in_{name}_dram", a.shape, _mybir.dt.from_np(a.dtype), kind="ExternalInput").ap())
    shape, dtype = _OUT
    args.append(nc.dram_tensor("out_0_dram", shape, _mybir.dt.from_np(_np.dtype(dtype)), kind="ExternalOutput").ap())
    build(nc, *args)
    r = _run(nc, [arrays], core_ids=[0])
    return r.results[0]["out_0_dram"]
```

```python
import concourse.bass as bass
from concourse import mybir
from contextlib import ExitStack


B, N, D, H, HD = 8, 256, 512, 16, 32
P = 128
NT = N // P
KC = D // P
G = 4
NG = H // G
NP = H // 2
S1, DK = 512, 16
ET, QT = N // P, S1 // P
SHIFT_ROW = 3 * HD
PAIR = 7 * HD
ODD = 3 * HD
EPS = 1e-6
NEG = 1e30

QKV_SLOTS = {0: 0, 1: 1, 2: 2, 3: 3, 4: 4, 5: 5}
STACK_SLOTS = {6: (0, 1), 7: (2, 3), 8: (4, 5), 9: (6, 7), 12: (8, 9), 13: (10, 11)}
STACK3_SLOTS = {0: (12, 13), 1: (14, 15)}
MAX_SLOTS = {8: (0, 1), 9: (2, 3), 10: (None, 4), 11: (5, 6), 12: (7,), 14: (None, 8, 9), 15: (10, 11)}
MAX3_SLOTS = {2: (None, 12), 3: (13,), 4: (14,), 5: (15,)}
MAX_T_SLOTS = {6: 1, 14: 0}
XT_SLOTS = {10: 0, 11: 1}
WOUT_SLOTS = {6: 0, 7: 1}
PROJ1_SLOT = 8
V1T_SLOT = 10
SCORE1_SLOTS = {10: 0, 11: 1, 12: 2, 13: 3}
E1T_SLOTS = {12: 0, 13: 1, 14: 2, 15: 3}
PV1_SLOTS = {13: 0, 14: 1, 15: 2}
SQUARE_SLOTS = {1: 0, 2: 1, 3: 2, 4: 3}
NORM_SLOTS = {2: 0, 3: 1, 4: 2, 5: 3}
HI_SLOTS = {3: 0, 4: 1, 5: 2, 6: 3}
O_SPLIT_SLOTS = {8: 0, 11: 1, 13: 2}
PLACE_SLOT = 14

F32 = mybir.dt.float32
F32R = mybir.dt.float32r
ACT = mybir.ActivationFunctionType
ALU = mybir.AluOpType
AX = mybir.AxisListType


def at(batch, per_batch, more):
    return batch * per_batch + more


def wait(eng, sem, value):
    if not isinstance(value, int) or value > 0:
        eng.wait_ge(sem, value)


def maxima_of(slot, k, batch, slots):
    heads = slots.get(slot, ())[k:k + 1] if batch is not None else ()
    return [h for h in heads if h is not None]


def settle(eng, count, batch):
    if not isinstance(batch, int):
        eng.sem_inc(count, 1)


def f32(ap):
    return ap.bitcast(F32)


def build(nc, x, cond, W_emb, b_emb, g_norm, W_qkv, g_q, g_k, W_out, L1_Wq, L1_Wk, L1_Wv, L1_Wo, out):
    ctx = ExitStack()
    with ctx:
        def sb(name, shape, dt=F32, where=ctx):
            return where.enter_context(nc.sbuf_tensor(name, shape, dt))

        def sem(name):
            return ctx.enter_context(nc.semaphore(name))

        wqkv_hi = sb("wqkv_hi", [P, KC, 3 * D], F32R)
        wqkv_lo = sb("wqkv_lo", [P, KC, 3 * D], F32R)
        wout_hi = sb("wout_hi", [P, KC, D], F32R)
        wout_lo = sb("wout_lo", [P, KC, D], F32R)
        ident_r = sb("ident_r", [P, P], F32R)
        ident = ident_r[:].bitcast(F32)
        gain_bc = sb("gain_bc", [P, HD])
        eps_col = sb("eps_col", [P, 1])
        cond_T = sb("cond_T", [P, B, KC])
        biasgain_T = sb("biasgain_T", [P, 12])
        mod_all = sb("mod_all", [P, B, 2 * KC])
        mod_cur = sb("mod_cur", [P, 2 * KC])
        w1 = sb("w1", [P, ET, 64 + DK])
        wo1 = sb("wo1", [2 * DK, N])[:]

        staging = ExitStack()
        gq_bc = sb("gq_bc", [P, HD], F32, staging)
        gk_bc = sb("gk_bc", [P, HD], F32, staging)
        w_emb_in = sb("w_emb_in", [P, KC, 2 * D], F32, staging)
        w_qkv_in = sb("w_qkv_in", [P, KC, 3 * D], F32, staging)
        rows_in = sb("rows_in", [12, P], F32, staging)
        cond_in = sb("cond_in", [B, D], F32, staging)
        mod_rows = sb("mod_rows", [B, 2 * D], F32, staging)
        staging.close()

        qk_split = sb("qk_split", [P, 2, NT, H, 3 * HD], F32R)
        q_stack = sb("q_stack", [SHIFT_ROW + 1, H, N], F32R)
        k_stack = sb("k_stack", [SHIFT_ROW + 1, H, N], F32R)
        qk_raw = sb("qk_raw", [P, NT, 2, D])
        o_t = sb("o_t", [2 * HD, N])
        o_hi = sb("o_hi", [P, NG, N], F32R)
        o_lo = sb("o_lo", [P, NG, N], F32R)
        v_raw = sb("v_raw", [P, NT, D])
        e = [sb(f"e{k}", [P, NT, N]) for k in range(2)]
        head_ms = sb("head_ms", [P, 4, H])
        head_y = sb("head_y", [P, 4, H])
        head_t = sb("head_t", [P, H])
        x_in = sb("x_in", [P, NT, D])
        x_ms = sb("x_ms", [P, NT])
        x_y = sb("x_y", [P, NT])
        x_t = sb("x_t", [P, NT])
        xn_T = sb("xn_T", [P, KC, N])
        squares = [xn_T[:, 2 * k:2 * k + 2].rearrange("p c n -> p (c n)") for k in range(2)]
        xn_hi = sb("xn_hi", [P, KC, N], F32R)
        xn_lo = sb("xn_lo", [P, KC, N], F32R)
        v_pad = sb("v_pad", [P, NT, NP, PAIR])
        maxima = sb("maxima", [P, 2, NT, H // 2])
        shift_T = [sb(f"shift_T{k}", [H, P], F32R) for k in range(2)]
        o_n = [sb(f"o_n{k}", [P, N]) for k in range(2)]
        ident_zero = o_n[0][:, 0:P]
        late_staging = ExitStack()
        wo1_in = sb("wo1_in", [2 * DK, H, N], F32, late_staging)
        w_out_in = sb("w_out_in", [P, KC, D], F32, late_staging)
        w1_in = sb("w1_in", [P, 3, ET, DK], F32, late_staging)
        late_staging.close()
        x1 = sb("x1", [P, NT, D])
        mask_bc = sb("mask_bc", [P, S1])
        pad_bias = sb("pad_bias", [P, S1])
        q1 = sb("q1", [96, S1], F32R)[:]
        k1 = sb("k1", [96, S1], F32R)[:]
        head1_T = sb("head1_T", [2 * DK, S1])[:]
        kv1 = sb("kv1", [64 + DK, S1])
        sums1 = kv1[0:4 * DK]
        v1 = sb("v1", [P, QT, P], F32R)
        e1 = [sb(f"e1_{k}", [P, S1]) for k in range(2)]
        min1 = sb("min1", [P, QT])
        e1_hi = sb("e1_hi", [P, QT, P], F32R)
        e1_lo = sb("e1_lo", [P, QT, P], F32R)

        def bank(name):
            return ctx.enter_context(nc.psum_tensor(name, [P, 512], F32))
        ps_logit = [bank(f"ps_logit{k}") for k in range(2)]
        ps_max = [bank(f"ps_max{k}") for k in range(2)]
        ps_o = bank("ps_o")
        ps_a, ps_b, ps_c = bank("ps_a"), bank("ps_b"), bank("ps_c")

        s_cond, s_rows, s_wout, s_wo1, s_w1, s_gains = map(
            sem, ["s_cond", "s_rows", "s_wout", "s_wo1", "s_w1", "s_gains"])
        s_wemb = [sem(f"s_wemb{k}") for k in range(KC)]
        s_wqkv = [sem(f"s_wqkv{k}") for k in range(KC)]
        s_x, s_resid, s_last_resid, s_mask, s_out = map(sem, ["s_x", "s_resid", "s_last_resid", "s_mask", "s_out"])
        s_shift = [sem(f"s_shift{k}") for k in range(2)]
        s_const, s_ident, s_condT, s_condT_sb, s_mod_ps, s_mod_b, s_mod, s_wsplit, s_w1sb, s_wo1sb, s_gain = map(
            sem, ["s_const", "s_ident", "s_condT", "s_condT_sb", "s_mod_ps", "s_mod_b", "s_mod", "s_wsplit",
                  "s_w1sb", "s_wo1sb", "s_gain"])
        s_mod_rows, s_modT = sem("s_mod_rows"), sem("s_modT")
        s_whi, s_ones, s_ones1, s_wdiag = sem("s_whi"), sem("s_ones"), sem("s_ones1"), sem("s_wdiag")
        p_xT, p_qkv, p_stack, p_max, p_maxT, p_logit, p_o, p_wout = map(
            sem, ["p_xT", "p_qkv", "p_stack", "p_max", "p_maxT", "p_logit", "p_o", "p_wout"])
        p_proj1, p_vT, p_score1, p_eT, p_o1, p_out1 = map(
            sem, ["p_proj1", "p_vT", "p_score1", "p_eT", "p_o1", "p_out1"])
        a_xms, a_xln, a_xy, a_xnT, a_raw, a_sq, a_ln, a_y, a_v, a_hi, a_stack = map(
            sem, ["a_xms", "a_xln", "a_xy", "a_xnT", "a_raw", "a_sq", "a_ln", "a_y", "a_v", "a_hi", "a_stack"])
        a_e, a_oln, a_oy, a_ohi = map(sem, ["a_e", "a_oln", "a_oy", "a_ohi"])
        a_q1, a_vT, a_k1hi, a_v1, a_e1, a_e1hi, a_sums = map(
            sem, ["a_q1", "a_vT", "a_k1hi", "a_v1", "a_e1", "a_e1hi", "a_sums"])
        v_ms, v_nt, v_y, v_qkn, v_stack, v_max, v_shift, v_oy, v_o, v_x1 = map(
            sem, ["v_ms", "v_nt", "v_y", "v_qkn", "v_stack", "v_max", "v_shift", "v_oy", "v_o", "v_x1"])
        v_q1, v_k1, v_v1, v_score1, v_e1lo, v_head1, v_x2 = map(
            sem, ["v_q1", "v_k1", "v_v1", "v_score1", "v_e1lo", "v_head1", "v_x2"])
        v_k1lo = sem("v_k1lo")
        g_mod, g_xhi, g_xlo, g_kgain, g_split, g_olo = map(
            sem, ["g_mod", "g_xhi", "g_xlo", "g_kgain", "g_split", "g_olo"])
        g_vpad, g_xn, g_x = map(sem, ["g_vpad", "g_xn", "g_x"])
        g_pad0, g_pad = map(sem, ["g_pad0", "g_pad"])
        passed_pool, passed_sp, passed_dve, passed_pe = map(
            sem, ["passed_pool", "passed_sp", "passed_dve", "passed_pe"])

        block = ctx.enter_context(nc.Block())

        def steps(eng, step):
            step(None, None, None, None, 0)
            step(None, None, None, 0, 1)
            step(None, None, 0, 1, 2)
            step(None, 0, 1, 2, 3)
            with eng.Fori(2, B - 2) as i:
                step(i - 2, i - 1, i, i + 1, i + 2)
            step(B - 4, B - 3, B - 2, B - 1, None)
            step(B - 3, B - 2, B - 1, None, None)
            step(B - 2, B - 1, None, None, None)
            step(B - 1, None, None, None, None)

        def qkv_bank(f, j):
            return "ac"[j % 2] if isinstance(f, int) and f == 0 else "a"

        def residual(batch):
            return x_in if isinstance(batch, int) and batch == B - 1 else x1

        @block.sync
        def _(sp):
            sp.dma_start(cond_in[:], cond).then_inc(s_cond, 16)
            sp.dma_start(rows_in[0:8, :], b_emb.rearrange("(c p) -> c p", p=P)).then_inc(s_rows, 16)
            sp.dma_start(rows_in[8:12, :], g_norm.rearrange("(c p) -> c p", p=P)).then_inc(s_rows, 16)
            w_emb_v = W_emb.rearrange("(c p) n -> p c n", p=P)

            def load_x(n):
                if not isinstance(n, int) or n > 0:
                    sp.wait_ge(p_xT, at(n, 2, 0))
                settle(sp, passed_sp, n)
                sp.dma_start(x_in[:], x[n].rearrange("(t p) d -> p t d", p=P)).then_inc(s_x, 16)

            def load_weights():
                for c in range(KC):
                    sp.dma_start(w_emb_in[:, c], w_emb_v[:, c]).then_inc(s_wemb[c], 16)
                w_qkv_v = W_qkv.rearrange("(c p) n -> p c n", p=P)
                for c in range(KC):
                    sp.dma_start(w_qkv_in[:, c], w_qkv_v[:, c]).then_inc(s_wqkv[c], 16)
                sp.dma_start(gq_bc[:], g_q.partition_broadcast(P)).then_inc(s_gains, 16)
                sp.dma_start(gk_bc[:], g_k.partition_broadcast(P)).then_inc(s_gains, 16)
                sp.dma_start(w_out_in[:], W_out.rearrange("(c p) n -> p c n", p=P)).then_inc(s_wout, 16)
                for k in range(2):
                    sp.dma_start(wo1_in[k * DK:(k + 1) * DK],
                                 L1_Wo.rearrange("(j i) n -> i j n", i=DK)).then_inc(s_wo1, 16)
                for k, w in enumerate((L1_Wq, L1_Wk, L1_Wv)):
                    sp.dma_start(w1_in[:, k], w[1].rearrange("(e p) d -> p e d", p=P)).then_inc(s_w1, 16)

            def shift_rows(half, batch):
                wait(sp, v_shift, at(batch, 2, half + 1))
                settle(sp, passed_sp, batch)
                h0 = half * (H // 2)
                wait(sp, p_logit, at(batch, H, -(H // 2)) if half == 0 else at(batch, H, 0))
                settle(sp, passed_sp, batch)
                for t in range(NT):
                    sp.dma_start(
                        f32(q_stack[SHIFT_ROW:SHIFT_ROW + 1, h0:h0 + H // 2, t * P:(t + 1) * P]),
                        f32(shift_T[half][t * (H // 2):(t + 1) * (H // 2), :]),
                    ).then_inc(s_shift[half], 16)

            def step(r, l, b, f, n):
                if n is not None:
                    load_x(n)
                    if isinstance(n, int) and n == 0:
                        load_weights()
                if l is not None and isinstance(l, int) and l == B - 1:
                    sp.wait_ge(p_xT, 2 * B)
                    sp.dma_start(residual(l)[:], x[l].rearrange("(t p) d -> p t d", p=P)).then_inc(s_last_resid, 16)
                if l is not None and isinstance(l, int) and l == 0:
                    sp.wait_ge(s_wsplit, KC + 1)
                    sp.wait_ge(s_wo1sb, 1)
                    sp.wait_ge(s_w1sb, 3)
                if l is not None:
                    wait(sp, v_head1, at(l, 12, 0))
                    settle(sp, passed_sp, l)
                    wait(sp, v_k1, at(l, 1, 0))
                    settle(sp, passed_sp, l)
                    wait(sp, g_pad, at(l, 1, 0))
                    settle(sp, passed_sp, l)
                    sp.dma_start(mask_bc[:], cond[l].partition_broadcast(P)).then_inc(s_mask, 16)
                if r is not None:
                    sp.wait_ge(v_x2, at(r, 2, 2))
                    settle(sp, passed_sp, r)
                    sp.dma_start(out[r].rearrange("(t p) d -> p t d", p=P), residual(r)[:]).then_inc(s_out, 16)
                if l is not None and not (isinstance(l, int) and l == B - 1):
                    wait(sp, s_out, at(l, 16, 0))
                    settle(sp, passed_sp, l)
                    sp.dma_start(x1[:], x[l].rearrange("(t p) d -> p t d", p=P)).then_inc(s_resid, 16)
                if b is not None:
                    shift_rows(1, b)
                if f is not None:
                    shift_rows(0, f)

            steps(sp, step)
            sp.wait_ge(s_out, 16 * B)

        @block.gpsimd
        def _(pool):
            g = nc.gpsimd
            g.memset(ident_zero, 0.0).then_inc(s_const, 1)
            g.memset(w1[:], 0.0).then_inc(s_const, 1)
            g.memset(eps_col[:], EPS).then_inc(s_const, 1)
            g.memset(v_pad[:], 0.0).then_inc(s_const, 1)
            pool.wait_ge(s_const, 4)
            g.affine_select(out=ident_r[:], in_=ident_zero, compare_op=ALU.not_equal, fill=1.0, base=0,
                            pattern=[[-1, P]], channel_multiplier=1).then_inc(s_ident, 1)
            for k in (2, 6):
                g.memset(v_pad[:, :, :, k * HD:(k + 1) * HD], 1.0).then_inc(s_const, 1)

            def copy(dst, src):
                return g.tensor_scalar(dst, src, 1.0, 0.0, ALU.mult, ALU.add)

            def gains():
                pool.wait_ge(s_gains, 32)
                g.tensor_tensor(gain_bc[:], gq_bc[:], gk_bc[:], ALU.mult).then_inc(s_gain, 1)
                pool.wait_ge(s_gain, 1)
                g.tensor_scalar(gain_bc[:], gain_bc[:], HD ** -0.5, 0.0, ALU.mult, ALU.add).then_inc(s_gain, 1)
                pool.wait_ge(s_gain, 2)

            def stack_ones():
                pool.wait_ge(s_mod_ps, 2 * KC)
                pool.wait_ge(s_wsplit, KC)
                g.memset(f32(k_stack[SHIFT_ROW:SHIFT_ROW + 1, :, :]), 1.0).then_inc(s_ones, 1)
                pool.wait_ge(s_ones, 1)

            def out_diagonal():
                pool.wait_ge(s_wout, 16)
                for c in range(KC):
                    block_c = w_out_in[:, c, c * P:(c + 1) * P]
                    g.tensor_tensor(block_c, block_c, ident, ALU.add).then_inc(s_wdiag, 1)

            def layer1_weights():
                pool.wait_ge(s_w1, 48)
                for k in range(3):
                    g.tensor_copy(w1[:, :, 32 * k:32 * k + DK], w1_in[:, k]).then_inc(s_w1sb, 1)

            def modulation(n):
                wait(pool, a_xnT, at(n, 4, 0))
                settle(pool, passed_pool, n)
                pool.wait_ge(s_mod, 2)
                g.tensor_copy(mod_cur[:], mod_all[:, n]).then_inc(g_mod, 1)

            def x_normalise(n):
                pool.wait_ge(a_xy, at(n, 1, 1))
                settle(pool, passed_pool, n)
                g.tensor_tensor(x_t[:], x_y[:], x_y[:], ALU.mult).then_inc(g_xn, 1)
                g.tensor_scalar(x_ms[:], x_ms[:], 1.0, EPS, ALU.mult, ALU.add).then_inc(g_xn, 1)
                pool.wait_ge(g_xn, at(n, 5, 2))
                g.tensor_tensor(x_t[:], x_ms[:], x_t[:], ALU.mult).then_inc(g_xn, 1)
                pool.wait_ge(g_xn, at(n, 5, 3))
                settle(pool, passed_pool, n)
                g.tensor_scalar(x_t[:], x_t[:], -0.5, 1.5, ALU.mult, ALU.add).then_inc(g_xn, 1)
                pool.wait_ge(g_xn, at(n, 5, 4))
                g.tensor_tensor(x_y[:], x_y[:], x_t[:], ALU.mult).then_inc(g_xn, 1)
                pool.wait_ge(g_xn, at(n, 5, 5))
                settle(pool, passed_pool, n)
                for t in range(NT):
                    g.tensor_scalar(x_in[:, t], x_in[:, t], x_y[:, t:t + 1], 0.0, ALU.mult, ALU.add).then_inc(g_x, 1)

            def x_split(n):
                pool.wait_ge(a_xnT, at(n, 4, 4))
                settle(pool, passed_pool, n)
                if not isinstance(n, int) or n > 0:
                    pool.wait_ge(p_qkv, at(n, 6, 0))
                    settle(pool, passed_pool, n)
                copy(xn_hi[:], xn_T[:]).then_inc(g_xhi, 1)
                pool.wait_ge(g_xhi, at(n, 1, 1))
                g.tensor_tensor(xn_lo[:], xn_T[:], f32(xn_hi[:]), ALU.subtract).then_inc(g_xlo, 1)

            def v_place(f, part):
                pool.wait_ge(a_v, at(f, 2, 2))
                settle(pool, passed_pool, f)
                wait(pool, p_o, at(f, H, -4) if part == 0 else at(f, H, 0))
                settle(pool, passed_pool, f)
                pairs = slice(0, 6) if part == 0 else slice(6, NP)
                for t in range(NT):
                    src = v_raw[:, t].rearrange("p (m k d) -> p m k d", k=2, d=HD)
                    for k in range(2):
                        ins = copy(v_pad[:, t, pairs, 4 * k * HD:(4 * k + 1) * HD], src[:, pairs, k])
                ins.then_inc(g_vpad, 1)

            def k_gain(f, t):
                pool.wait_ge(a_sq, at(f, 4, 2 * t + 2))
                k = qk_raw[:, t, 1].rearrange("p (h d) -> p h d", d=HD)
                gain = gain_bc[:].unsqueeze(1).to_broadcast([P, H, HD])
                g.tensor_tensor(k, k, gain, ALU.mult).then_inc(g_kgain, 1)

            def split(f, j):
                t, k = j // 2, j % 2
                dst = qk_split[:, k, t]
                val = qk_raw[:, t, k].rearrange("p (h d) -> p h d", d=HD)
                lo, again = (1, 2) if k == 0 else (2, 1)
                pool.wait_ge(a_hi, at(f, 4, j + 1))
                g.tensor_tensor(dst[:, :, lo * HD:(lo + 1) * HD], val, f32(dst[:, :, 0:HD]),
                                ALU.subtract).then_inc(g_split, 1)
                copy(dst[:, :, again * HD:(again + 1) * HD], f32(dst[:, :, 0:HD])).then_inc(g_split, 1)

            def o_lo_part(b, grp):
                pool.wait_ge(a_ohi, at(b, NG, grp + 1))
                g.tensor_tensor(o_lo[:, grp], o_n[grp % 2][:], f32(o_hi[:, grp]), ALU.subtract).then_inc(g_olo, 1)

            def mask_bias(l):
                pool.wait_ge(s_mask, at(l, 16, 16))
                settle(pool, passed_pool, l)
                wait(pool, v_score1, at(l, 4, 0))
                settle(pool, passed_pool, l)
                g.tensor_scalar(pad_bias[:], mask_bc[:], -1.0, 1.0, ALU.mult, ALU.add).then_inc(g_pad0, 1)
                pool.wait_ge(g_pad0, at(l, 1, 1))
                settle(pool, passed_pool, l)
                g.tensor_scalar(pad_bias[:], pad_bias[:], NEG, 0.0, ALU.mult, ALU.add).then_inc(g_pad, 1)

            def step(r, l, b, f, n):
                if f is not None and isinstance(f, int) and f == 0:
                    gains()
                    stack_ones()
                if n is not None and isinstance(n, int) and n == 0:
                    x_normalise(n)
                    modulation(n)
                for s in range(H):
                    if b is not None and s == 0:
                        v_place(b, 1)
                    if l is not None and s == 1:
                        o_lo_part(l, NG - 1)
                    if f is not None and s in (2, 4):
                        k_gain(f, s // 2 - 1)
                    if f is not None and s in HI_SLOTS:
                        split(f, HI_SLOTS[s])
                    if l is not None and s == 4:
                        mask_bias(l)
                    if b is not None and s in O_SPLIT_SLOTS:
                        o_lo_part(b, O_SPLIT_SLOTS[s])
                    if n is not None and s == 8 and not (isinstance(n, int) and n == 0):
                        x_normalise(n)
                        modulation(n)
                    if n is not None and s == 12:
                        x_split(n)
                    if f is not None and s == PLACE_SLOT:
                        v_place(f, 0)
                if f is not None and isinstance(f, int) and f == 0:
                    out_diagonal()
                    layer1_weights()

            steps(pool, step)

        @block.scalar
        def _(act):
            a = nc.scalar
            a.preload_act_table_set("natural_log_exp_and_others")
            act.wait_ge(s_const, 6)

            def weights_hi(c):
                act.wait_ge(s_wqkv[c], 16)
                a.activation(wqkv_hi[:, c], w_qkv_in[:, c], ACT.Copy).then_inc(s_whi, 1)

            def wout_hi_part():
                act.wait_ge(s_wdiag, KC)
                a.activation(wout_hi[:], w_out_in[:], ACT.Copy).then_inc(s_whi, 1)

            def x_squares(n, t):
                act.wait_ge(s_x, at(n, 16, 16))
                wait(act, g_x, at(n, 2, 0))
                wait(act, v_ms, at(n, 4, 0))
                a.activation(xn_T[:, 2 * t:2 * t + 2].rearrange("p c n -> p (c n)"), x_in[:, t], ACT.Square,
                             scale=D ** -0.5, accum_out=x_ms[:, t:t + 1]).then_inc(a_xms, 1)

            def x_rsqrt(n):
                act.wait_ge(a_xms, at(n, 2, 2))
                wait(act, g_x, at(n, 2, 0))
                a.activation(x_y[:], x_ms[:], ACT.Ln, bias=eps_col[:]).then_inc(a_xln, 1)
                act.wait_ge(a_xln, at(n, 1, 1))
                a.activation(x_y[:], x_y[:], ACT.Exp, scale=-0.5).then_inc(a_xy, 1)

            def modulate(n, j):
                act.wait_ge(g_mod, at(n, 1, 1))
                act.wait_ge(p_xT, at(n, 2, j + 1))
                for c in (2 * j, 2 * j + 1):
                    a.activation(xn_T[:, c], ps_a[:, (c % 2) * N:(c % 2 + 1) * N], ACT.Identity,
                                 scale=mod_cur[:, c:c + 1], bias=mod_cur[:, KC + c:KC + c + 1]).then_inc(a_xnT, 1)

            def qk_out(f, j):
                t, k = j // 2, j % 2
                act.wait_ge(p_qkv, at(f, 6, j + 1))
                wait(act, g_split, at(f, 8, 0))
                ps = {"a": ps_a, "c": ps_c}[qkv_bank(f, j)]
                a.activation(qk_raw[:, t, k], ps[:], ACT.Copy).then_inc(a_raw, 1)

            def qk_square(f, j):
                t, k = j // 2, j % 2
                act.wait_ge(a_raw, at(f, 4, j + 1))
                if j < 2:
                    act.wait_ge(g_xlo, at(f, 1, 1))
                else:
                    act.wait_ge(v_ms, at(f, 4, j - 1))
                a.activation(squares[j % 2], qk_raw[:, t, k], ACT.Square, scale=HD ** -0.5).then_inc(a_sq, 1)

            def qk_rsqrt(f, j):
                act.wait_ge(v_ms, at(f, 4, j + 1))
                wait(act, v_qkn, at(f, 4, 0))
                a.activation(head_y[:, j], head_ms[:, j], ACT.Ln, bias=eps_col[:]).then_inc(a_ln, 1)
                act.wait_ge(a_ln, at(f, 4, j + 1))
                a.activation(head_y[:, j], head_y[:, j], ACT.Exp, scale=-0.5).then_inc(a_y, 1)

            def qk_hi(f, j):
                t, k = j // 2, j % 2
                act.wait_ge(v_qkn, at(f, 4, j + 1))
                wait(act, p_stack, at(f, 4 * NG, 0))
                a.activation(qk_split[:, k, t, :, 0:HD], qk_raw[:, t, k].rearrange("p (h d) -> p h d", d=HD),
                             ACT.Copy).then_inc(a_hi, 1)

            def v_out(f, t):
                act.wait_ge(p_qkv, at(f, 6, 5 + t))
                wait(act, g_vpad, at(f, 2, 0))
                ps = {"a": ps_a, "c": ps_c}[qkv_bank(f, 4 + t)]
                a.activation(v_raw[:, t], ps[:], ACT.Copy).then_inc(a_v, 1)

            def stack_out(f, j, ps):
                grp, k, t = j // 4, j // 2 % 2, j % 2
                dst = (q_stack, k_stack)[k]
                act.wait_ge(p_stack, at(f, 4 * NG, j + 1))
                a.activation(dst[0:SHIFT_ROW, grp * G:(grp + 1) * G, t * P:(t + 1) * P],
                             ps[0:SHIFT_ROW, :].rearrange("p (h n) -> p h n", h=G), ACT.Copy).then_inc(a_stack, 1)

            def exp(b, h):
                act.wait_ge(p_logit, at(b, H, h + 1))
                wait(act, p_o, at(b, H, h - 1))
                a.activation(e[h % 2][:].rearrange("p t n -> p (t n)"), ps_logit[h % 2][:],
                             ACT.Exp).then_inc(a_e, 1)

            def o_reciprocal(b, pair):
                grp, k = pair // 2, pair % 2
                act.wait_ge(p_o, at(b, H, 2 * pair + 2))
                wait(act, g_olo, at(b, NG, grp - 1))
                o = o_n[grp % 2][k * 2 * HD:(k + 1) * 2 * HD, :]
                a.activation(o, ps_o[2 * HD:4 * HD, 0:N], ACT.Ln).then_inc(a_oln, 1)
                act.wait_ge(a_oln, at(b, NP, pair + 1))
                a.activation(o, o, ACT.Exp, scale=-1.0).then_inc(a_oy, 1)

            def o_hi_part(b, grp):
                act.wait_ge(v_o, at(b, NP, 2 * grp + 2))
                wait(act, p_wout, at(b, 2, 0))
                a.activation(o_hi[:, grp], o_n[grp % 2][:], ACT.Copy).then_inc(a_ohi, 1)

            def q1_out(l):
                act.wait_ge(p_proj1, at(l, 1, 1))
                wait(act, p_score1, at(l, 4, 0))
                a.activation(q1[0:32], ps_c[0:32, :], ACT.Copy, scale=-(DK ** -0.5))
                a.activation(q1[64:96], ps_c[0:32, :], ACT.Copy, scale=-(DK ** -0.5)).then_inc(a_q1, 1)

            def v1_out(l):
                wait(act, p_vT, at(l, 1, 0))
                a.activation(kv1[64:64 + DK], ps_c[64:64 + DK, :], ACT.Copy).then_inc(a_vT, 1)

            def k1_hi(l):
                act.wait_ge(v_k1, at(l, 1, 1))
                a.activation(k1[0:32], kv1[32:64], ACT.Copy)
                a.activation(k1[32:64], kv1[32:64], ACT.Copy).then_inc(a_k1hi, 1)

            def v1_hi(l):
                act.wait_ge(p_vT, at(l, 1, 1))
                wait(act, p_o1, at(l, 4, 0))
                a.activation(v1[:, :, 0:DK], ps_b[:, 0:QT * DK].rearrange("p (t d) -> p t d", d=DK),
                             ACT.Copy).then_inc(a_v1, 1)

            def exp1(l, q):
                act.wait_ge(v_score1, at(l, 4, q + 1))
                a.activation(e1[q % 2][:], e1[q % 2][:], ACT.Exp, scale=-1.0,
                             bias=min1[:, q:q + 1]).then_inc(a_e1, 1)

            def e1_hi_out(l, q):
                act.wait_ge(p_eT, at(l, 4, q + 1))
                wait(act, p_o1, at(l, 4, q))
                a.activation(e1_hi[:].rearrange("p t n -> p (t n)"), ps_b[:], ACT.Copy).then_inc(a_e1hi, 1)

            def sums1_out(l, q):
                act.wait_ge(p_o1, at(l, 4, q + 1))
                if q == 0:
                    act.wait_ge(v_k1lo, at(l, 1, 1))
                a.activation(sums1[:, q * P:(q + 1) * P], ps_c[0:4 * DK, 0:P], ACT.Copy).then_inc(a_sums, 1)

            def step(r, l, b, f, n):
                if n is not None and isinstance(n, int) and n == 0:
                    x_squares(n, 0)
                    x_squares(n, 1)
                    x_rsqrt(n)
                    weights_hi(0)
                    weights_hi(1)
                if f is not None and isinstance(f, int) and f == 0:
                    act.wait_ge(s_gain, 2)
                for s in range(H):
                    if b is not None:
                        exp(b, s)
                    if s == 0 and l is not None:
                        o_reciprocal(l, NP - 1)
                    if b is not None and s % 2 == 0 and s >= 2:
                        o_reciprocal(b, s // 2 - 1)
                    if r is not None and s == 0:
                        sums1_out(r, 3)
                    if l is not None and s in PV1_SLOTS:
                        sums1_out(l, PV1_SLOTS[s])
                    if f is not None and s in NORM_SLOTS:
                        qk_rsqrt(f, NORM_SLOTS[s])
                    if f is not None and s in SQUARE_SLOTS:
                        qk_square(f, SQUARE_SLOTS[s])
                    if l is not None and s == 1:
                        o_hi_part(l, NG - 1)
                    if f is not None and s in HI_SLOTS:
                        qk_hi(f, HI_SLOTS[s])
                    if n is not None and not (isinstance(n, int) and n == 0):
                        if s in (5, 6):
                            x_squares(n, s - 5)
                        if s == 7:
                            x_rsqrt(n)
                    if f is not None and QKV_SLOTS.get(s, 9) < 4:
                        qk_out(f, QKV_SLOTS[s])
                    if f is not None and 4 <= QKV_SLOTS.get(s, 9) < 6:
                        v_out(f, QKV_SLOTS[s] - 4)
                    if b is not None and s in STACK3_SLOTS:
                        stack_out(b, STACK3_SLOTS[s][0], ps_b)
                    if f is not None and s in STACK_SLOTS:
                        stack_out(f, STACK_SLOTS[s][0], ps_a)
                    if l is not None:
                        if s == PROJ1_SLOT:
                            q1_out(l)
                        if s == 9:
                            v1_out(l)
                            k1_hi(l)
                        if s == V1T_SLOT:
                            v1_hi(l)
                        if s in E1T_SLOTS:
                            e1_hi_out(l, E1T_SLOTS[s])
                        if s - 1 in SCORE1_SLOTS:
                            exp1(l, SCORE1_SLOTS[s - 1])
                    if b is not None and s in O_SPLIT_SLOTS:
                        o_hi_part(b, O_SPLIT_SLOTS[s])
                    if n is not None and s in XT_SLOTS:
                        modulate(n, XT_SLOTS[s])
                if n is not None and isinstance(n, int) and n == 0:
                    weights_hi(2)
                    weights_hi(3)
                if f is not None and isinstance(f, int) and f == 0:
                    wout_hi_part()

            steps(act, step)

        @block.vector
        def _(dve):
            v = nc.vector
            dve.wait_ge(s_condT, 1)
            v.tensor_copy(cond_T[:].rearrange("p b c -> p c b"),
                          ps_a[:, 0:KC * B].rearrange("p (c b) -> p c b", b=B)).then_inc(s_condT_sb, 1)
            v.tensor_copy(biasgain_T[:], ps_a[:, 64:76]).then_inc(s_condT_sb, 1)

            def all_modulations():
                dve.wait_ge(s_condT_sb, 2)
                dve.wait_ge(s_mod_ps, 2 * KC)
                for half in range(2):
                    v.tensor_copy(mod_rows[:, half * D:(half + 1) * D],
                                  (ps_b, ps_c)[half][0:B, :]).then_inc(s_mod_rows, 1)
                dve.wait_ge(s_modT, 1)
                v.tensor_tensor(mod_all[:].rearrange("p b c -> p c b"),
                                ps_b[:, 0:2 * KC * B].rearrange("p (c b) -> p c b", b=B),
                                biasgain_T[:, 0:8].unsqueeze(2).to_broadcast([P, 8, B]), ALU.add).then_inc(s_mod_b, 1)
                dve.wait_ge(s_mod_b, 1)
                v.tensor_scalar(mod_all[:, :, 0:KC], mod_all[:, :, 0:KC], 1.0, None, ALU.add).then_inc(s_mod, 1)
                dve.wait_ge(s_mod, 1)
                v.tensor_tensor(mod_all[:, :, 0:KC], mod_all[:, :, 0:KC],
                                biasgain_T[:, 8:12].unsqueeze(1).to_broadcast([P, B, KC]), ALU.mult).then_inc(s_mod, 1)

            def weights_lo(c):
                dve.wait_ge(s_whi, c + 1)
                v.tensor_tensor(wqkv_lo[:, c], w_qkv_in[:, c], f32(wqkv_hi[:, c]), ALU.subtract).then_inc(s_wsplit, 1)

            def more_weights():
                dve.wait_ge(s_whi, KC + 1)
                v.tensor_tensor(wout_lo[:], w_out_in[:], f32(wout_hi[:]), ALU.subtract).then_inc(s_wsplit, 1)
                dve.wait_ge(s_wo1, 32)
                v.tensor_reduce(wo1, wo1_in[:].rearrange("i j n -> i n j"), AX.X, ALU.add).then_inc(s_wo1sb, 1)
                dve.wait_ge(s_wsplit, KC + 1)
                dve.wait_ge(s_wo1sb, 1)
                dve.wait_ge(s_w1sb, 3)
                v.memset(f32(v1[:, :, 2 * DK:]), 1.0).then_inc(s_ones1, 1)

            def newton(y, ms, t, count, seen):
                v.tensor_tensor(t, y, y, ALU.mult).then_inc(count, 1)
                dve.wait_ge(count, seen(1))
                v.scalar_tensor_tensor(out=t, in0=ms, scalar=EPS, in1=t, op0=ALU.add, op1=ALU.mult).then_inc(count, 1)
                dve.wait_ge(count, seen(2))
                v.tensor_scalar(t, t, -0.5, 1.5, ALU.mult, ALU.add).then_inc(count, 1)
                dve.wait_ge(count, seen(3))
                return v.tensor_tensor(y, y, t, ALU.mult)

            def mean_squares(f, j):
                dve.wait_ge(a_sq, at(f, 4, j + 1))
                v.tensor_reduce(head_ms[:, j], squares[j % 2].rearrange("p (h d) -> p h d", d=HD),
                                AX.X, ALU.add).then_inc(v_ms, 1)

            def qk_norm(f, j):
                t, k = j // 2, j % 2
                dve.wait_ge(a_y, at(f, 4, j + 1))
                newton(head_y[:, j], head_ms[:, j], head_t[:], v_nt, lambda m: at(f, 12, 3 * j + m)).then_inc(v_y, 1)
                dve.wait_ge(v_y, at(f, 4, j + 1))
                dve.wait_ge(a_raw, at(f, 4, j + 1))
                if k == 1:
                    dve.wait_ge(g_kgain, at(f, 2, t + 1))
                val = qk_raw[:, t, k].rearrange("p (h d) -> p h d", d=HD)
                v.tensor_tensor(val, val, head_y[:, j].unsqueeze(2).to_broadcast([P, H, HD]),
                                ALU.mult).then_inc(v_qkn, 1)

            def stack_out(f, j, ps):
                grp, k, t = j // 4, j // 2 % 2, j % 2
                dst = (q_stack, k_stack)[k]
                dve.wait_ge(p_stack, at(f, 4 * NG, j + 1))
                v.tensor_copy(dst[0:SHIFT_ROW, grp * G:(grp + 1) * G, t * P:(t + 1) * P],
                              ps[0:SHIFT_ROW, :].rearrange("p (h n) -> p h n", h=G)).then_inc(v_stack, 1)

            def row_max(b, h):
                dve.wait_ge(p_max, at(b, H, h + 1))
                v.tensor_reduce(maxima[:, h // 8, :, h % 8], ps_max[h % 2][:].rearrange("p (t n) -> p t n", t=NT),
                                AX.X, ALU.max).then_inc(v_max, 1)

            def shift_out(batch, half):
                dve.wait_ge(p_maxT, at(batch, 2, half + 1))
                wait(dve, s_shift[half], at(batch, 32, 0))
                v.tensor_scalar(shift_T[half][:], (ps_a, ps_b)[half][0:H, 0:P], -1.0, None,
                                ALU.mult).then_inc(v_shift, 1)

            def o_norm(b, pair):
                grp, k = pair // 2, pair % 2
                dve.wait_ge(a_oy, at(b, NP, pair + 1))
                o = o_n[grp % 2][k * 2 * HD:(k + 1) * 2 * HD, :]
                sums, dens = ps_o[0:2 * HD, 0:N], ps_o[2 * HD:4 * HD, 0:N]
                wait(dve, v_o, at(b, NP, pair))
                v.scalar_tensor_tensor(out=o_t[:], in0=dens, scalar=-1.0, in1=o, op0=ALU.mult,
                                       op1=ALU.mult).then_inc(v_oy, 1)
                v.tensor_tensor(o, sums, o, ALU.mult).then_inc(v_oy, 1)
                dve.wait_ge(v_oy, at(b, 2 * NP, 2 * pair + 2))
                v.scalar_tensor_tensor(out=o, in0=o_t[:], scalar=2.0, in1=o, op0=ALU.add,
                                       op1=ALU.mult).then_inc(v_o, 1)

            def x1_out(l, t):
                dve.wait_ge(p_wout, at(l, 2, t + 1))
                if isinstance(l, int) and l == B - 1:
                    dve.wait_ge(s_last_resid, 16)
                else:
                    dve.wait_ge(s_resid, at(l, 16, 16))
                v.tensor_tensor(residual(l)[:, t], ps_c[:], residual(l)[:, t], ALU.add).then_inc(v_x1, 1)

            def q1_lo(l):
                dve.wait_ge(a_q1, at(l, 1, 1))
                dve.wait_ge(a_vT, at(l, 1, 1))
                v.scalar_tensor_tensor(out=q1[32:64], in0=ps_c[0:32, :], scalar=-(DK ** -0.5),
                                       in1=f32(q1[0:32]), op0=ALU.mult, op1=ALU.subtract).then_inc(v_q1, 1)

            def k1_mask(l):
                dve.wait_ge(p_proj1, at(l, 1, 1))
                dve.wait_ge(s_mask, at(l, 16, 16))
                wait(dve, v_head1, at(l, 12, 0))
                v.tensor_tensor(kv1[32:64], ps_c[32:64, :], mask_bc[32:64, :], ALU.mult).then_inc(v_k1, 1)

            def k1_lo(l):
                dve.wait_ge(a_k1hi, at(l, 1, 1))
                v.tensor_tensor(k1[64:96], kv1[32:64], f32(k1[32:64]), ALU.subtract).then_inc(v_k1lo, 1)

            def v1_lo(l):
                dve.wait_ge(a_v1, at(l, 1, 1))
                v.tensor_tensor(v1[:, :, DK:2 * DK], ps_b[:, 0:QT * DK].rearrange("p (t d) -> p t d", d=DK),
                                f32(v1[:, :, 0:DK]), ALU.subtract).then_inc(v_v1, 1)

            def score1(l, q):
                dve.wait_ge(p_score1, at(l, 4, q + 1))
                dve.wait_ge(g_pad, at(l, 1, 1))
                wait(dve, p_eT, at(l, 4, q - 1) if q >= 2 else at(l, 4, 0))
                settle(dve, passed_dve, l)
                v.tensor_tensor_reduce(out=e1[q % 2][:], in0=ps_c[:], in1=pad_bias[:], scale=1.0, scalar=3e38,
                                       op0=ALU.add, op1=ALU.min, accum_out=min1[:, q:q + 1]).then_inc(v_score1, 1)

            def e1_lo_out(l, q):
                dve.wait_ge(a_e1hi, at(l, 4, q + 1))
                v.tensor_tensor(e1_lo[:].rearrange("p t n -> p (t n)"), ps_b[:],
                                f32(e1_hi[:]).rearrange("p t n -> p (t n)"), ALU.subtract).then_inc(v_e1lo, 1)

            def head1_out(l, q):
                cols = slice(q * P, (q + 1) * P)
                dve.wait_ge(a_sums, at(l, 4, q + 1))
                wait(dve, p_out1, at(l, 2, 0))
                v.reciprocal(head1_T[:, cols], sums1[2 * DK:4 * DK, cols]).then_inc(v_head1, 1)
                dve.wait_ge(v_head1, at(l, 12, 3 * q + 1))
                v.tensor_tensor(head1_T[:, cols], head1_T[:, cols], sums1[0:2 * DK, cols],
                                ALU.mult).then_inc(v_head1, 1)
                dve.wait_ge(v_head1, at(l, 12, 3 * q + 2))
                v.tensor_tensor(head1_T[:, cols], head1_T[:, cols], mask_bc[0:2 * DK, cols],
                                ALU.mult).then_inc(v_head1, 1)

            def x2_out(r, t):
                dve.wait_ge(p_out1, at(r, 2, t + 1))
                v.tensor_tensor(residual(r)[:, t], (ps_b, ps_c)[t][:], residual(r)[:, t], ALU.add).then_inc(v_x2, 1)

            def step(r, l, b, f, n):
                if n is not None and isinstance(n, int) and n == 0:
                    all_modulations()
                    weights_lo(0)
                    weights_lo(1)
                    weights_lo(2)
                    weights_lo(3)
                for s in range(H):
                    for h in maxima_of(s, 0, f, MAX_SLOTS):
                        row_max(f, h)
                    if s == 6 and b is not None:
                        shift_out(b, 1)
                    if l is not None and s == 0:
                        o_norm(l, NP - 1)
                    if b is not None and s % 2 == 0 and s >= 2:
                        o_norm(b, s // 2 - 1)
                    for h in maxima_of(s, 0, b, MAX3_SLOTS):
                        row_max(b, h)
                    if r is not None and s == 2:
                        head1_out(r, 3)
                    if f is not None and s in NORM_SLOTS:
                        qk_norm(f, NORM_SLOTS[s])
                    if f is not None and s in SQUARE_SLOTS:
                        mean_squares(f, SQUARE_SLOTS[s])
                    if l is not None and s in WOUT_SLOTS:
                        x1_out(l, WOUT_SLOTS[s])
                    if r is not None and s == 3:
                        x2_out(r, 0)
                        x2_out(r, 1)
                    if l is not None:
                        if s == PROJ1_SLOT:
                            k1_mask(l)
                        if s == V1T_SLOT:
                            v1_lo(l)
                        if s in E1T_SLOTS and s in SCORE1_SLOTS:
                            score1(l, SCORE1_SLOTS[s])
                        if s in E1T_SLOTS:
                            e1_lo_out(l, E1T_SLOTS[s])
                    if s == 14 and f is not None:
                        shift_out(f, 0)
                    for h in maxima_of(s, 1, b, MAX3_SLOTS):
                        row_max(b, h)
                    for h in maxima_of(s, 1, f, MAX_SLOTS):
                        row_max(f, h)
                    if l is not None and s in SCORE1_SLOTS and s not in E1T_SLOTS:
                        score1(l, SCORE1_SLOTS[s])
                    if l is not None and s in (14, 15):
                        head1_out(l, s - 14)
                    if b is not None and s in STACK3_SLOTS:
                        stack_out(b, STACK3_SLOTS[s][1], ps_c)
                    if f is not None and s in STACK_SLOTS:
                        stack_out(f, STACK_SLOTS[s][1], ps_b if s < 12 else ps_a)
                    for h in maxima_of(s, 2, f, MAX_SLOTS):
                        row_max(f, h)
                    if l is not None and s == 9:
                        q1_lo(l)
                        k1_lo(l)
                    if r is not None and s == 0:
                        head1_out(r, 2)
                if f is not None and isinstance(f, int) and f == 0:
                    more_weights()

            steps(dve, step)

        @block.tensor
        def _(pe):
            mm, tr = nc.tensor.matmul, nc.tensor.transpose
            pe.wait_ge(s_ident, 1)
            pe.wait_ge(s_cond, 16)
            pe.wait_ge(s_rows, 32)
            for c in range(KC):
                tr(ps_a[:, c * B:(c + 1) * B], cond_in[:, c * P:(c + 1) * P], ident[0:B, 0:B])
            tr(ps_a[:, 64:76], rows_in[0:12, :], ident[0:12, 0:12]).then_inc(s_condT, 1)

            def modulation_product():
                pe.wait_ge(s_condT_sb, 2)
                for c in range(KC):
                    pe.wait_ge(s_wemb[c], 16)
                    for half in range(2):
                        mm((ps_b, ps_c)[half][0:B, :], cond_T[:, :, c], w_emb_in[:, c, half * D:(half + 1) * D],
                           start=(c == 0), stop=(c == KC - 1)).then_inc(s_mod_ps, 1)
                pe.wait_ge(s_mod_rows, 2)
                for m in range(2 * KC):
                    ins = tr(ps_b[:, m * B:(m + 1) * B], mod_rows[:, m * P:(m + 1) * P], ident[0:B, 0:B])
                ins.then_inc(s_modT, 1)

            def product3(ps, a_hi_, a_lo_, w_hi_, w_lo_, toks, cols, part, first=False):
                todo = [(a, w, c) for c in range(KC) for a, w in ((a_hi_, w_hi_), (a_lo_, w_hi_), (a_hi_, w_lo_))]
                half = len(todo) // 2
                for n in range(part * half, (part + 1) * half):
                    a, w, c = todo[n]
                    if first and n % 3 == 0:
                        pe.wait_ge(s_wsplit, c + 1)
                    ins = mm(ps[:], a[:, c, toks], w[:, c, cols], start=(n == 0), stop=(n == len(todo) - 1))
                return ins

            freed = {"a": (s_condT_sb, 2), "b": (s_mod_b, 1), "c": (s_mod_rows, 2)}

            def use(name, reader, value):
                if freed[name] is not None:
                    wait(pe, *freed[name])
                freed[name] = (reader, value)
                return {"a": ps_a, "b": ps_b, "c": ps_c}[name]

            def x_T(n, j):
                ps = use("a", a_xnT, at(n, 4, 2 * j + 2))
                pe.wait_ge(g_x, at(n, 2, 2))
                for c in range(2):
                    for t in range(NT):
                        ins = tr(ps[:, c * N + t * P:c * N + (t + 1) * P],
                                 x_in[:, t, (2 * j + c) * P:(2 * j + c + 1) * P], ident)
                ins.then_inc(p_xT, 1)

            def qkv_product(f, j, part):
                t = j // 2 if j < 4 else j - 4
                k = j % 2 if j < 4 else 2
                if part == 0:
                    use(qkv_bank(f, j), *((a_raw, at(f, 4, j + 1)) if j < 4 else (a_v, at(f, 2, j - 3))))
                    pe.wait_ge(g_xlo, at(f, 1, 1))
                ps = {"a": ps_a, "c": ps_c}[qkv_bank(f, j)]
                ins = product3(ps, xn_hi, xn_lo, wqkv_hi, wqkv_lo, slice(t * P, (t + 1) * P),
                               slice(k * D, (k + 1) * D), part, first=isinstance(f, int) and f == 0 and j == 0)
                if part == 1:
                    ins.then_inc(p_qkv, 1)

            def out_product(l, t, part):
                if part == 0:
                    use("c", v_x1, at(l, 2, t + 1))
                    pe.wait_ge(g_olo, at(l, NG, NG))
                ins = product3(ps_c, o_hi, o_lo, wout_hi, wout_lo, slice(t * P, (t + 1) * P), slice(0, D), part)
                if part == 1:
                    ins.then_inc(p_wout, 1)

            def stack(f, j):
                grp, k, t = j // 4, j // 2 % 2, j % 2
                name = ("ab", "ab", "aa", "bc")[grp][j % 2]
                ps = use(name, (a_stack, v_stack)[j % 2], at(f, 8, j // 2 + 1))
                pe.wait_ge(g_split, at(f, 8, 2 * (2 * t + k) + 2))
                for h in range(G):
                    ins = tr(ps[0:SHIFT_ROW, h * P:(h + 1) * P].bitcast(F32R), qk_split[:, k, t, grp * G + h, :],
                             ident_r[:])
                ins.then_inc(p_stack, 1)

            def max_logits(b, h):
                wait(pe, v_max, at(b, H, h - 1))
                pe.wait_ge(a_stack, at(b, 8, 2 * (h // G + 1)))
                pe.wait_ge(v_stack, at(b, 8, 2 * (h // G + 1)))
                for t in range(NT):
                    ins = mm(ps_max[h % 2][:, t * N:(t + 1) * N], q_stack[0:SHIFT_ROW, h, t * P:(t + 1) * P],
                             k_stack[0:SHIFT_ROW, h, :], start=True, stop=True)
                ins.then_inc(p_max, 1)

            def max_T(batch, half):
                ps = use("ab"[half], v_shift, at(batch, 2, half + 1))
                pe.wait_ge(v_max, at(batch, H, (half + 1) * (H // 2)))
                tr(ps[0:H, 0:P], maxima[:, half].rearrange("p t h -> p (t h)"), ident).then_inc(p_maxT, 1)

            def logits(b, h):
                wait(pe, a_e, at(b, H, h - 1))
                pe.wait_ge(s_shift[h // 8], at(b, 32, 32))
                for t in range(NT):
                    ins = mm(ps_logit[h % 2][:, t * N:(t + 1) * N], k_stack[:, h, t * P:(t + 1) * P],
                             q_stack[:, h, :], start=True, stop=True)
                ins.then_inc(p_logit, 1)

            def weighted_v(b, h):
                pair, odd = h // 2, h % 2
                if odd == 0:
                    wait(pe, v_oy, at(b, 2 * NP, 2 * pair))
                pe.wait_ge(a_e, at(b, H, h + 1))
                pe.wait_ge(g_vpad, at(b, 2, 1 if pair < 6 else 2))
                for t in range(NT):
                    lhsT = v_pad[:, t, pair, odd * ODD:odd * ODD + P]
                    ins = mm(ps_o[:, 0:N], lhsT, e[h % 2][:, t, :],
                             start=(odd == 0 and t == 0), stop=(odd == 1 and t == NT - 1))
                ins.then_inc(p_o, 1)

            def project1(l):
                ps = use("c", v_q1, at(l, 1, 1))
                pe.wait_ge(v_x1, at(l, 2, 2))
                for t in range(ET):
                    ins = mm(ps[0:64 + DK, :], w1[:, t, :], residual(l)[:, t, :], start=(t == 0), stop=(t == ET - 1))
                ins.then_inc(p_proj1, 1)

            def v1_T(l):
                ps = use("b", v_v1, at(l, 1, 1))
                pe.wait_ge(a_vT, at(l, 1, 1))
                settle(pe, passed_pe, l)
                for t in range(QT):
                    ins = tr(ps[:, t * DK:(t + 1) * DK], kv1[64:64 + DK, t * P:(t + 1) * P],
                             ident[64:64 + DK, 64:64 + DK])
                ins.then_inc(p_vT, 1)

            def scores1(l, q):
                ps = use("c", v_score1, at(l, 4, q + 1))
                pe.wait_ge(v_q1, at(l, 1, 1))
                pe.wait_ge(v_k1lo, at(l, 1, 1))
                mm(ps[:], q1[:, q * P:(q + 1) * P], k1, start=True, stop=True).then_inc(p_score1, 1)

            def e1_transposes(l, q):
                ps = use("b", v_e1lo, at(l, 4, q + 1))
                pe.wait_ge(a_e1, at(l, 4, q + 1))
                for t in range(QT):
                    ins = tr(ps[:, t * P:(t + 1) * P], e1[q % 2][:, t * P:(t + 1) * P], ident)
                ins.then_inc(p_eT, 1)

            def weighted_v1(l, q):
                ps = use("c", a_sums, at(l, 4, q + 1))
                pe.wait_ge(v_e1lo, at(l, 4, q + 1))
                pe.wait_ge(v_v1, at(l, 1, 1))
                for t in range(QT):
                    mm(ps[:, 0:P], v1[:, t, :], e1_hi[:, t, :], start=(t == 0), stop=False)
                    ins = mm(ps[:, 0:P], v1[:, t, :], e1_lo[:, t, :], start=False, stop=(t == QT - 1))
                ins.then_inc(p_o1, 1)

            def out1(r, t):
                ps = use("bc"[t], v_x2, at(r, 2, t + 1))
                pe.wait_ge(v_head1, at(r, 12, 12))
                mm(ps[:], wo1[:, t * P:(t + 1) * P], head1_T, start=True, stop=True).then_inc(p_out1, 1)

            def step(r, l, b, f, n):
                if n is not None and isinstance(n, int) and n == 0:
                    modulation_product()
                if b is not None:
                    freed["a"] = (v_shift, at(b, 2, 1))
                if r is not None:
                    freed["b"] = (v_e1lo, at(r, 4, 4))
                    freed["c"] = (a_sums, at(r, 4, 3))
                if b is not None and isinstance(b, int) and b == 0:
                    pe.wait_ge(s_ones, 1)
                if l is not None and isinstance(l, int) and l == 0:
                    pe.wait_ge(s_wsplit, KC + 1)
                    pe.wait_ge(s_w1sb, 3)
                    pe.wait_ge(s_ones1, 1)
                    pe.wait_ge(s_wo1sb, 1)
                for s in range(H):
                    def products(part):
                        if f is not None and s in QKV_SLOTS:
                            qkv_product(f, QKV_SLOTS[s], part)
                        if l is not None and s in WOUT_SLOTS:
                            out_product(l, WOUT_SLOTS[s], part)

                    def stacks(k):
                        if b is not None and s in STACK3_SLOTS:
                            stack(b, STACK3_SLOTS[s][k])
                        if f is not None and s in STACK_SLOTS:
                            stack(f, STACK_SLOTS[s][k])

                    def maxima_products(k):
                        for h in maxima_of(s, k, b, MAX3_SLOTS):
                            max_logits(b, h)
                        for h in maxima_of(s, k, f, MAX_SLOTS):
                            max_logits(f, h)

                    if b is not None:
                        logits(b, s)
                    if b is not None and s >= 1:
                        weighted_v(b, s - 1)
                    if l is not None and s == 0:
                        weighted_v(l, H - 1)
                    if b is not None and MAX_T_SLOTS.get(s) == 1:
                        max_T(b, 1)
                    products(0)
                    maxima_products(0)
                    if r is not None and s == 0:
                        weighted_v1(r, 3)
                    if l is not None and s in PV1_SLOTS:
                        weighted_v1(l, PV1_SLOTS[s])
                    if f is not None and MAX_T_SLOTS.get(s) == 0:
                        max_T(f, 0)
                    products(1)
                    if l is not None and s == PROJ1_SLOT:
                        project1(l)
                    stacks(0)
                    if l is not None and s == V1T_SLOT:
                        v1_T(l)
                    if l is not None and s in E1T_SLOTS:
                        e1_transposes(l, E1T_SLOTS[s])
                    if r is not None and s == 3:
                        out1(r, 0)
                        out1(r, 1)
                    maxima_products(1)
                    if l is not None:
                        if s in SCORE1_SLOTS:
                            scores1(l, SCORE1_SLOTS[s])
                    stacks(1)
                    maxima_products(2)
                    if n is not None and s in XT_SLOTS:
                        x_T(n, XT_SLOTS[s])

            steps(pe, step)


_INS = ['x', 'cond_2048', 'L0_cond_W_emb', 'L0_cond_b_emb', 'L0_cond_g_norm', 'L0_cond_W_qkv', 'L0_cond_g_q',
        'L0_cond_g_k', 'L0_cond_W_out', 'L1_cond_Wq', 'L1_cond_Wk', 'L1_cond_Wv', 'L1_cond_Wo']
_OUT = ((B, N, D), 'float32')


def kernel(**inputs):
    import numpy as _np
    import concourse.bacc as _bacc
    from concourse import mybir as _mybir
    from concourse.bass_utils import run_bass_kernel_spmd as _run

    nc = _bacc.Bacc("TRN2", target_bir_lowering=False, num_devices=1)
    arrays, args = {}, []
    for name in _INS:
        a = _np.ascontiguousarray(inputs[name])
        arrays[f"in_{name}_dram"] = a
        args.append(nc.dram_tensor(f"in_{name}_dram", a.shape, _mybir.dt.from_np(a.dtype), kind="ExternalInput").ap())
    shape, dtype = _OUT
    args.append(nc.dram_tensor("out_0_dram", shape, _mybir.dt.from_np(_np.dtype(dtype)), kind="ExternalOutput").ap())
    build(nc, *args)
    r = _run(nc, [arrays], core_ids=[0])
    return r.results[0]["out_0_dram"]
```
